# Optimizing a Trainium2 kernel written in Bass

```python
import numpy as np
import jax
import jax.numpy as jnp

def _softmax(x, axis=-1):
    return jax.nn.softmax(x, axis=axis)

def _gelu(x):
    return jax.nn.gelu(x, approximate=True)

def _silu(x):
    return jax.nn.silu(x)

def _sigmoid(x):
    return jax.nn.sigmoid(x)

def _layernorm(x, axis=-1, eps=1e-05):
    m = jnp.mean(x, axis=axis, keepdims=True)
    v = jnp.var(x, axis=axis, keepdims=True)
    return (x - m) / jnp.sqrt(v + eps)

def _scatter_add(tgt, idx, src, axis=0):
    return tgt.at[idx].add(src)

def _segment_sum(src, seg, n):
    return jax.ops.segment_sum(src, seg, n)
kernel_name = 'mk_perceiver_d1_seqx_r2_b0910c'

def setup_inputs(seed: int=0):
    np.random.seed(seed)
    _w = jnp.asarray

    def _rec_inputs():
        import jax
        import jax.numpy as jnp
        _rk = jax.random.key(seed)
        x = -0.0005207 + 1.001 * jax.random.normal(jax.random.fold_in(_rk, 1), (2, 128, 512), jnp.float32)
        _lenS = 128 - jax.random.randint(jax.random.fold_in(_rk, 7), (2,), 0, max(1, 128 // 4) + 1, jnp.int32)
        _lenS2 = 2048 - jax.random.randint(jax.random.fold_in(_rk, 8), (2,), 0, max(1, 2048 // 4) + 1, jnp.int32)
        _ctx_1024P = jax.random.normal(jax.random.fold_in(_rk, 11), (2, 16, 512), jnp.float32)
        _ctx_1024c = jax.random.dirichlet(jax.random.fold_in(_rk, 511), 0.3 * jnp.ones((16,), jnp.float32), (2, 2048))
        _ctx_1024t = jnp.einsum('bsk,bkd->bsd', _ctx_1024c, _ctx_1024P)
        _ctx_1024t = _ctx_1024t * jax.lax.rsqrt(jnp.mean(jnp.square(_ctx_1024t)) + 1e-12) * 0.953939
        ctx_1024 = -0.000514642 + 1.00011 * (_ctx_1024t + 0.3 * jax.random.normal(jax.random.fold_in(_rk, 611), (2, 2048, 512), jnp.float32))
        return (x, ctx_1024)
    x, ctx_1024 = _rec_inputs()

    def _L0_xattn_setup():
        import jax, jax.numpy as jnp
        import numpy as np
        EMBED_DIM = 512
        NUM_HEADS = 16
        HEAD_DIM = EMBED_DIM // NUM_HEADS
        WINDOW = 64

        def apply_rope(x):
            B, H, S, d = x.shape
            half = d // 2
            pos = jnp.arange(S, dtype=x.dtype)
            freqs = 1.0 / 10000.0 ** (jnp.arange(half, dtype=x.dtype) / half)
            ang = pos[:, None] * freqs[None, :]
            cos, sin = (jnp.cos(ang), jnp.sin(ang))
            x1, x2 = (x[..., :half], x[..., half:])
            return jnp.concatenate([x1 * cos - x2 * sin, x1 * sin + x2 * cos], axis=-1)

        def _forward(query, key, value, q_w, q_b, k_w, k_b, v_w, v_b, o_w, o_b):
            B, S_q, D = query.shape
            S_k = key.shape[1]
            H, d, W = (NUM_HEADS, HEAD_DIM, WINDOW)
            q = (query @ q_w.T + q_b).reshape(B, S_q, H, d).transpose(0, 2, 1, 3)
            k = (key @ k_w.T + k_b).reshape(B, S_k, H, d).transpose(0, 2, 1, 3)
            v = (value @ v_w.T + v_b).reshape(B, S_k, H, d).transpose(0, 2, 1, 3)
            q = apply_rope(q) * d ** (-0.5)
            k = apply_rope(k)
            q_pos = jnp.arange(S_q)[:, None]
            offsets = jnp.arange(-W, 1)[None, :]
            idx = q_pos + offsets
            local_mask = (idx < 0) | (idx >= S_k)
            gidx = jnp.clip(idx, 0, S_k - 1)
            k_win = k[:, :, gidx, :]
            v_win = v[:, :, gidx, :]
            scores = jnp.einsum('bhqd,bhqwd->bhqw', q, k_win)
            mask = local_mask[None, None, :, :]
            scores = jnp.where(mask, -jnp.inf, scores)
            m = jnp.max(scores, axis=-1, keepdims=True)
            m = jnp.where(jnp.isfinite(m), m, 0.0)
            e = jnp.exp(scores - m)
            denom = jnp.sum(e, axis=-1, keepdims=True)
            probs = jnp.where(denom > 0, e / jnp.where(denom > 0, denom, 1.0), 0.0)
            ctx = jnp.einsum('bhqw,bhqwd->bhqd', probs, v_win)
            ctx = ctx.transpose(0, 2, 1, 3).reshape(B, S_q, D)
            return ctx @ o_w.T + o_b
        key = jax.random.key(seed)
        ks = jax.random.split(key, 12)
        B, S, D = (1, 1024, EMBED_DIM)
        scale = 1.0 / np.sqrt(D)
        inp = {'query': jax.random.normal(ks[0], (B, S, D), jnp.float32), 'key': jax.random.normal(ks[1], (B, S, D), jnp.float32), 'value': jax.random.normal(ks[2], (B, S, D), jnp.float32), 'q_w': jax.random.normal(ks[3], (D, D), jnp.float32) * scale, 'q_b': jax.random.normal(ks[4], (D,), jnp.float32) * 0.01, 'k_w': jax.random.normal(ks[5], (D, D), jnp.float32) * scale, 'k_b': jax.random.normal(ks[6], (D,), jnp.float32) * 0.01, 'v_w': jax.random.normal(ks[7], (D, D), jnp.float32) * scale, 'v_b': jax.random.normal(ks[8], (D,), jnp.float32) * 0.01, 'o_w': jax.random.normal(ks[9], (D, D), jnp.float32) * scale, 'o_b': jax.random.normal(ks[10], (D,), jnp.float32) * 0.01}
        return inp
    _L0_xattn_all = _L0_xattn_setup()
    _L0_xattn_in = {k: v for k, v in _L0_xattn_all.items() if k in ('q_w', 'q_b', 'k_w', 'k_b', 'v_w', 'v_b', 'o_w', 'o_b')}
    del _L0_xattn_all

    def _L0_attn_setup():
        import jax, jax.numpy as jnp
        import numpy as np
        B, S, D, H = (2, 1024, 512, 16)
        Dh = D // H
        C = 2
        EPS = 1e-06
        LN_EPS = 1e-05

        def _rope_cache(seq_len, dh):
            half = dh // 2
            inv_freq = 1.0 / 10000.0 ** (jnp.arange(0, 2 * half, 2, dtype=jnp.float32) / dh)
            t = jnp.arange(seq_len, dtype=jnp.float32)
            freqs = t[:, None] * inv_freq[None, :]
            return (jnp.cos(freqs), jnp.sin(freqs))

        def _apply_rope(u, cos, sin):
            half = u.shape[-1] // 2
            c = cos[None, :, None, :]
            s = sin[None, :, None, :]
            u1, u2 = (u[..., :half], u[..., half:2 * half])
            return jnp.concatenate([u1 * c - u2 * s, u1 * s + u2 * c], axis=-1)

        def _deltanet_fwd(x, Wq, Wk, Wv, Wbeta, bbeta, Wo, bo, ln_gamma, ln_beta):
            Bn, Sn, Dm = x.shape
            q = (x @ Wq).reshape(Bn, Sn, H, Dh)
            k = (x @ Wk).reshape(Bn, Sn, H, Dh)
            v = (x @ Wv).reshape(Bn, Sn, H, Dh)
            cos, sin = _rope_cache(Sn, Dh)
            q = _apply_rope(q, cos, sin)
            k = _apply_rope(k, cos, sin)
            phi = lambda u: jax.nn.elu(u) + 1.0
            q_phi, k_phi = (phi(q), phi(k))
            beta = jnp.clip(jax.nn.sigmoid(x @ Wbeta + bbeta).reshape(Bn, Sn, H, C), 0.001, 0.999)

            def tm(u):
                return u.transpose(0, 2, 1, 3).reshape(Bn * H, Sn, -1).transpose(1, 0, 2)
            qs, ks_, vs, bs = (tm(q_phi), tm(k_phi), tm(v), tm(beta))
            BH = Bn * H
            M0 = jnp.zeros((BH, C, Dh, Dh), jnp.float32)
            Z0 = jnp.zeros((BH, C, Dh), jnp.float32)

            def step(carry, inp):
                M, Z = carry
                q_t, k_t, v_t, b_t = inp
                M = M * b_t[:, :, None, None] + (k_t[:, :, None] * v_t[:, None, :])[:, None]
                Z = Z * b_t[:, :, None] + k_t[:, None, :]
                num = jnp.einsum('bd,bcde->be', q_t, M)
                den = jnp.einsum('bd,bcd->b', q_t, Z) + EPS
                return ((M, Z), num / den[:, None])
            _, ys = jax.lax.scan(step, (M0, Z0), (qs, ks_, vs, bs))
            out = ys.transpose(1, 0, 2).reshape(Bn, H, Sn, Dh).transpose(0, 2, 1, 3).reshape(Bn, Sn, Dm)
            out = out @ Wo + bo
            h = x + out
            mu = jnp.mean(h, axis=-1, keepdims=True)
            var = jnp.mean((h - mu) ** 2, axis=-1, keepdims=True)
            return ln_gamma * (h - mu) / jnp.sqrt(var + LN_EPS) + ln_beta
        key = jax.random.key(seed)
        ks = jax.random.split(key, 8)
        w = 0.02
        x = jax.random.normal(ks[0], (B, S, D), jnp.float32)
        Wq = jax.random.normal(ks[1], (D, D), jnp.float32) * w
        Wk = jax.random.normal(ks[2], (D, D), jnp.float32) * w
        Wv = jax.random.normal(ks[3], (D, D), jnp.float32) * w
        Wbeta = jax.random.normal(ks[4], (D, H * C), jnp.float32) * w
        bbeta = jnp.full((H * C,), np.log(0.98 / 0.02), jnp.float32)
        Wo = jax.random.normal(ks[5], (D, D), jnp.float32) * w
        bo = jnp.zeros((D,), jnp.float32)
        ln_gamma = jnp.ones((D,), jnp.float32)
        ln_beta = jnp.zeros((D,), jnp.float32)
        return {'x': x, 'Wq': Wq, 'Wk': Wk, 'Wv': Wv, 'Wbeta': Wbeta, 'bbeta': bbeta, 'Wo': Wo, 'bo': bo, 'ln_gamma': ln_gamma, 'ln_beta': ln_beta}
    _L0_attn_all = _L0_attn_setup()
    _L0_attn_in = {k: v for k, v in _L0_attn_all.items() if k in ('Wq', 'Wk', 'Wv', 'Wbeta', 'bbeta', 'Wo', 'bo', 'ln_gamma', 'ln_beta')}
    del _L0_attn_all

    def _L0_ffn_setup():
        import jax, jax.numpy as jnp
        import numpy as np
        B, S, D, H, O, E, K = (4, 1024, 512, 1024, 512, 8, 2)
        key = jax.random.key(seed)
        ks = jax.random.split(key, 8)
        x = jax.random.normal(ks[0], (B, S, D), dtype=jnp.float32)
        gate_w = jax.random.uniform(ks[1], (E, D), dtype=jnp.float32, minval=-1, maxval=1) * np.sqrt(6.0 / D)
        gate_b = jnp.zeros((E,), dtype=jnp.float32)
        w1 = jax.random.uniform(ks[2], (E, D, H), dtype=jnp.float32, minval=-1, maxval=1) * np.sqrt(6.0 / D)
        b1 = jnp.zeros((E, H), dtype=jnp.float32)
        w2 = jax.random.uniform(ks[3], (E, H, O), dtype=jnp.float32, minval=-1, maxval=1) * np.sqrt(6.0 / H)
        b2 = jnp.zeros((E, O), dtype=jnp.float32)
        return {'x': x, 'gate_w': gate_w, 'gate_b': gate_b, 'w1': w1, 'b1': b1, 'w2': w2, 'b2': b2}
    _L0_ffn_all = _L0_ffn_setup()
    _L0_ffn_in = {k: v for k, v in _L0_ffn_all.items() if k in ('gate_w', 'gate_b', 'w1', 'b1', 'w2', 'b2')}
    del _L0_ffn_all
    return {'x': x, 'ctx_1024': ctx_1024, 'L0_xattn_q_w': _L0_xattn_in['q_w'], 'L0_xattn_q_b': _L0_xattn_in['q_b'], 'L0_xattn_k_w': _L0_xattn_in['k_w'], 'L0_xattn_k_b': _L0_xattn_in['k_b'], 'L0_xattn_v_w': _L0_xattn_in['v_w'], 'L0_xattn_v_b': _L0_xattn_in['v_b'], 'L0_xattn_o_w': _L0_xattn_in['o_w'], 'L0_xattn_o_b': _L0_xattn_in['o_b'], 'L0_attn_Wq': _L0_attn_in['Wq'], 'L0_attn_Wk': _L0_attn_in['Wk'], 'L0_attn_Wv': _L0_attn_in['Wv'], 'L0_attn_Wbeta': _L0_attn_in['Wbeta'], 'L0_attn_bbeta': _L0_attn_in['bbeta'], 'L0_attn_Wo': _L0_attn_in['Wo'], 'L0_attn_bo': _L0_attn_in['bo'], 'L0_attn_ln_gamma': _L0_attn_in['ln_gamma'], 'L0_attn_ln_beta': _L0_attn_in['ln_beta'], 'L0_ffn_gate_w': _L0_ffn_in['gate_w'], 'L0_ffn_gate_b': _L0_ffn_in['gate_b'], 'L0_ffn_w1': _L0_ffn_in['w1'], 'L0_ffn_b1': _L0_ffn_in['b1'], 'L0_ffn_w2': _L0_ffn_in['w2'], 'L0_ffn_b2': _L0_ffn_in['b2']}

def reference(x, ctx_1024, L0_xattn_q_w, L0_xattn_q_b, L0_xattn_k_w, L0_xattn_k_b, L0_xattn_v_w, L0_xattn_v_b, L0_xattn_o_w, L0_xattn_o_b, L0_attn_Wq, L0_attn_Wk, L0_attn_Wv, L0_attn_Wbeta, L0_attn_bbeta, L0_attn_Wo, L0_attn_bo, L0_attn_ln_gamma, L0_attn_ln_beta, L0_ffn_gate_w, L0_ffn_gate_b, L0_ffn_w1, L0_ffn_b1, L0_ffn_w2, L0_ffn_b2):
    import jax
    import jax.numpy as jnp

    def _L0_xattn_ref(query, key, value, q_w, q_b, k_w, k_b, v_w, v_b, o_w, o_b):
        import jax, jax.numpy as jnp
        import numpy as np
        EMBED_DIM = 512
        NUM_HEADS = 16
        HEAD_DIM = EMBED_DIM // NUM_HEADS
        WINDOW = 64

        def apply_rope(x):
            B, H, S, d = x.shape
            half = d // 2
            pos = jnp.arange(S, dtype=x.dtype)
            freqs = 1.0 / 10000.0 ** (jnp.arange(half, dtype=x.dtype) / half)
            ang = pos[:, None] * freqs[None, :]
            cos, sin = (jnp.cos(ang), jnp.sin(ang))
            x1, x2 = (x[..., :half], x[..., half:])
            return jnp.concatenate([x1 * cos - x2 * sin, x1 * sin + x2 * cos], axis=-1)

        def _forward(query, key, value, q_w, q_b, k_w, k_b, v_w, v_b, o_w, o_b):
            B, S_q, D = query.shape
            S_k = key.shape[1]
            H, d, W = (NUM_HEADS, HEAD_DIM, WINDOW)
            q = (query @ q_w.T + q_b).reshape(B, S_q, H, d).transpose(0, 2, 1, 3)
            k = (key @ k_w.T + k_b).reshape(B, S_k, H, d).transpose(0, 2, 1, 3)
            v = (value @ v_w.T + v_b).reshape(B, S_k, H, d).transpose(0, 2, 1, 3)
            q = apply_rope(q) * d ** (-0.5)
            k = apply_rope(k)
            q_pos = jnp.arange(S_q)[:, None]
            offsets = jnp.arange(-W, 1)[None, :]
            idx = q_pos + offsets
            local_mask = (idx < 0) | (idx >= S_k)
            gidx = jnp.clip(idx, 0, S_k - 1)
            k_win = k[:, :, gidx, :]
            v_win = v[:, :, gidx, :]
            scores = jnp.einsum('bhqd,bhqwd->bhqw', q, k_win)
            mask = local_mask[None, None, :, :]
            scores = jnp.where(mask, -jnp.inf, scores)
            m = jnp.max(scores, axis=-1, keepdims=True)
            m = jnp.where(jnp.isfinite(m), m, 0.0)
            e = jnp.exp(scores - m)
            denom = jnp.sum(e, axis=-1, keepdims=True)
            probs = jnp.where(denom > 0, e / jnp.where(denom > 0, denom, 1.0), 0.0)
            ctx = jnp.einsum('bhqw,bhqwd->bhqd', probs, v_win)
            ctx = ctx.transpose(0, 2, 1, 3).reshape(B, S_q, D)
            return ctx @ o_w.T + o_b
        return _forward(query, key, value, q_w, q_b, k_w, k_b, v_w, v_b, o_w, o_b)

    def _L0_attn_ref(x, Wq, Wk, Wv, Wbeta, bbeta, Wo, bo, ln_gamma, ln_beta):
        import jax, jax.numpy as jnp
        import numpy as np
        B, S, D, H = (2, 1024, 512, 16)
        Dh = D // H
        C = 2
        EPS = 1e-06
        LN_EPS = 1e-05

        def _rope_cache(seq_len, dh):
            half = dh // 2
            inv_freq = 1.0 / 10000.0 ** (jnp.arange(0, 2 * half, 2, dtype=jnp.float32) / dh)
            t = jnp.arange(seq_len, dtype=jnp.float32)
            freqs = t[:, None] * inv_freq[None, :]
            return (jnp.cos(freqs), jnp.sin(freqs))

        def _apply_rope(u, cos, sin):
            half = u.shape[-1] // 2
            c = cos[None, :, None, :]
            s = sin[None, :, None, :]
            u1, u2 = (u[..., :half], u[..., half:2 * half])
            return jnp.concatenate([u1 * c - u2 * s, u1 * s + u2 * c], axis=-1)

        def _deltanet_fwd(x, Wq, Wk, Wv, Wbeta, bbeta, Wo, bo, ln_gamma, ln_beta):
            Bn, Sn, Dm = x.shape
            q = (x @ Wq).reshape(Bn, Sn, H, Dh)
            k = (x @ Wk).reshape(Bn, Sn, H, Dh)
            v = (x @ Wv).reshape(Bn, Sn, H, Dh)
            cos, sin = _rope_cache(Sn, Dh)
            q = _apply_rope(q, cos, sin)
            k = _apply_rope(k, cos, sin)
            phi = lambda u: jax.nn.elu(u) + 1.0
            q_phi, k_phi = (phi(q), phi(k))
            beta = jnp.clip(jax.nn.sigmoid(x @ Wbeta + bbeta).reshape(Bn, Sn, H, C), 0.001, 0.999)

            def tm(u):
                return u.transpose(0, 2, 1, 3).reshape(Bn * H, Sn, -1).transpose(1, 0, 2)
            qs, ks_, vs, bs = (tm(q_phi), tm(k_phi), tm(v), tm(beta))
            BH = Bn * H
            M0 = jnp.zeros((BH, C, Dh, Dh), jnp.float32)
            Z0 = jnp.zeros((BH, C, Dh), jnp.float32)

            def step(carry, inp):
                M, Z = carry
                q_t, k_t, v_t, b_t = inp
                M = M * b_t[:, :, None, None] + (k_t[:, :, None] * v_t[:, None, :])[:, None]
                Z = Z * b_t[:, :, None] + k_t[:, None, :]
                num = jnp.einsum('bd,bcde->be', q_t, M)
                den = jnp.einsum('bd,bcd->b', q_t, Z) + EPS
                return ((M, Z), num / den[:, None])
            _, ys = jax.lax.scan(step, (M0, Z0), (qs, ks_, vs, bs))
            out = ys.transpose(1, 0, 2).reshape(Bn, H, Sn, Dh).transpose(0, 2, 1, 3).reshape(Bn, Sn, Dm)
            out = out @ Wo + bo
            h = x + out
            mu = jnp.mean(h, axis=-1, keepdims=True)
            var = jnp.mean((h - mu) ** 2, axis=-1, keepdims=True)
            return ln_gamma * (h - mu) / jnp.sqrt(var + LN_EPS) + ln_beta
        return _deltanet_fwd(x, Wq, Wk, Wv, Wbeta, bbeta, Wo, bo, ln_gamma, ln_beta)

    def _L0_ffn_ref(x, gate_w, gate_b, w1, b1, w2, b2):
        import jax, jax.numpy as jnp
        import numpy as np
        B, S, D, H, O, E, K = (4, 1024, 512, 1024, 512, 8, 2)
        logits = jnp.einsum('bsd,ed->bse', x, gate_w) + gate_b
        probs = jax.nn.softmax(logits, axis=-1)
        topk_vals, topk_idx = jax.lax.top_k(probs, K)
        h = jax.nn.relu(jnp.einsum('bsd,edh->bseh', x, w1) + b1)
        expert_out = jnp.einsum('bseh,eho->bseo', h, w2) + b2
        sel = jnp.take_along_axis(expert_out, topk_idx[..., None], axis=2)
        return jnp.sum(sel * topk_vals[..., None], axis=2)
    x = x + _L0_xattn_ref(_layernorm(x, axis=-1), ctx_1024, ctx_1024, L0_xattn_q_w, L0_xattn_q_b, L0_xattn_k_w, L0_xattn_k_b, L0_xattn_v_w, L0_xattn_v_b, L0_xattn_o_w, L0_xattn_o_b)
    x = x + _L0_attn_ref(_layernorm(x, axis=-1), L0_attn_Wq, L0_attn_Wk, L0_attn_Wv, L0_attn_Wbeta, L0_attn_bbeta, L0_attn_Wo, L0_attn_bo, L0_attn_ln_gamma, L0_attn_ln_beta)
    x = x + _L0_ffn_ref(_layernorm(x, axis=-1), L0_ffn_gate_w, L0_ffn_gate_b, L0_ffn_w1, L0_ffn_b1, L0_ffn_w2, L0_ffn_b2)
    return x

_drawn_inputs = setup_inputs


def setup_inputs(seed=0):
    import zlib

    import numpy as np

    out = dict(_drawn_inputs(seed))
    spreads = {'L0_attn_bbeta': (3.891820192337036, 0.6),
     'L0_attn_bo': (0.0, 0.1),
     'L0_attn_ln_gamma': (1.0, 0.2),
     'L0_attn_ln_beta': (0.0, 0.1),
     'L0_ffn_gate_b': (0.0, 0.1),
     'L0_ffn_b1': (0.0, 0.337),
     'L0_ffn_b2': (0.0, 0.335)}
    factors = {'L0_xattn_q_b': 8.0,
     'L0_xattn_k_b': 40.164,
     'L0_xattn_v_b': 5.081,
     'L0_xattn_o_b': 4.474,
     'L0_attn_Wq': 60.115,
     'L0_attn_Wk': 44.019,
     'L0_attn_Wbeta': 24.526}
    for name, (base, spread) in spreads.items():
        noise = np.random.default_rng([zlib.crc32(name.encode()), seed]).standard_normal(out[name].shape)
        drawn = base * np.exp(spread * noise) if base else spread * noise
        out[name] = jnp.asarray(drawn.astype(out[name].dtype))
    for name, factor in factors.items():
        out[name] = (out[name] * factor).astype(out[name].dtype)
    return out
```

```python
from contextlib import ExitStack

import concourse.bass as bass
from concourse import mybir

F32 = mybir.dt.float32
BF16 = mybir.dt.bfloat16
U32 = mybir.dt.uint32
ALU = mybir.AluOpType
ACT = mybir.ActivationFunctionType
AX = mybir.AxisListType

P = 128
NB = 2
D = 512
DC = D // P
H, HD = 16, 32
G = P // HD
WINDOW = 64
C = 2
E, FF = 8, 1024
FC = FF // P
RING = 4
LN_EPS, DEN_EPS = 1e-5, 1e-6
MASKED = -1e30


def build(nc, x, ctx_t, rope, wk, wv, wq, wo, aq, ak, av, ao, wbeta, bbeta, biases, norm_rows,
          gate_w, gate_b, w1, b1, w2, b2, out):
    with ExitStack() as ctx:
        def sb(name, shape, dt=F32):
            return ctx.enter_context(nc.sbuf_tensor(name, shape, dt))

        sems = {}

        def sem(name):
            if name not in sems:
                sems[name] = ctx.enter_context(nc.semaphore(name))
            return sems[name]

        bank = [ctx.enter_context(nc.psum_tensor(f"bank{i}", [P, D], F32)) for i in range(8)]

        first_w = [sb(f"first_w{i}", [P, 8 * D]) for i in range(2)]
        stage_w = [sb(f"stage_w{i}", [P, 8 * D]) for i in range(4)]
        proj = [stage_w[i // 2][:, (i % 2) * DC * D:(i % 2 + 1) * DC * D].rearrange("p (c n) -> p c n", c=DC)
                for i in range(8)]
        wk_s, wv_s, wq_s, wo_s, aq_s, ak_s, av_s, ao_s = proj
        wide = [sb(f"wide{i}", [P, 8 * D]) for i in range(2)]
        w1_ring = [first_w[0], stage_w[0], wide[0], stage_w[2]]
        w2_ring = [first_w[1], stage_w[1], wide[1], stage_w[3]]
        w1_s = [w[:, :].rearrange("p (c n) -> p c n", c=DC) for w in w1_ring]
        w2_s = [w[:, :].rearrange("p (c n) -> p c n", c=FC) for w in w2_ring]

        x_s = sb("x_s", [P, NB, D])
        ctx_s = sb("ctx_s", [P, DC, NB * P])
        rope_s = sb("rope_s", [P, 4, HD])
        bias_s = sb("bias_s", [1, 5, D])
        norm_s = sb("norm_s", [P, 2, D])
        wbeta_s = sb("wbeta_s", [P, DC, H * C])
        bbeta_s = sb("bbeta_s", [H * C, 1])
        gate_s = sb("gate_s", [P, DC, E])
        gateb_s = sb("gateb_s", [1, E])
        b1_s = sb("b1_s", [P, E, FC])
        b2_s = sb("b2_s", [E, D])

        ones_row = sb("ones_row", [1, P])
        ident = sb("ident", [P, P])
        ident_h = sb("ident_h", [P, P], BF16)
        band = sb("band", [P, DC, P], BF16)
        eye2 = sb("eye2", [P, NB, P])
        row_pick = sb("row_pick", [3 * H * C, H * C], BF16)
        iota8 = sb("iota8", [P, E])
        half_neg = sb("half_neg", [P, 1])

        bstat = sb("bstat", [P, NB, 6])
        mv = sb("mv", [P, 4, NB, 2])
        veps = sb("veps", [P, 4, NB])
        rstd = sb("rstd", [P, 4, NB])

        xn = sb("xn", [P, NB, D])
        tT = sb("tT", [P, DC, NB, P])
        rope_ab = sb("rope_ab", [P, 2, NB, D])
        rope_a, rope_b = rope_ab[:, 0], rope_ab[:, 1]
        qr = sb("qr", [P, NB, D])
        kr = sb("kr", [P, NB, D])
        qkT = sb("qkT", [P, 2, DC, NB, P])
        qT, kT = qkT[:, 0], qkT[:, 1]
        vv = sb("vv", [P, NB, H, HD + 1])
        den = sb("den", [P, NB, H])
        x1 = sb("x1", [P, NB, D])
        probs = wide[0][:, :].rearrange("p (b j c k) -> p b j c k", b=NB, j=G, c=DC)
        probsT = wide[1][:, :].rearrange("p (b j c k) -> p b j c k", b=NB, j=G, c=DC)
        decay = [w[:, :].rearrange("p (h n) -> p h n", h=H) for w in wide]
        negmax = sb("negmax", [P, NB, G, DC])
        beta_e = sb("beta_e", [H * C, NB, P])
        beta_r = sb("beta_r", [H * C, NB, P])
        beta_p = sb("beta_p", [3 * H * C, NB, P], BF16)
        mixed = qr
        mixedT = qT
        lg = sb("lg", [P, NB, E])
        lge = sb("lge", [P, NB, E])
        lmax = sb("lmax", [P, NB])
        lsum = sb("lsum", [P, NB])
        top8 = sb("top8", [P, NB, 8])
        top_i = sb("top_i", [P, NB, 8], U32)
        top_f = sb("top_f", [P, NB, 8])
        pick = sb("pick", [P, 2, NB, E])
        gatep = sb("gatep", [P, NB, E])
        gatepT = sb("gatepT", [E, NB, P])
        hid = [rope_ab[:, :].rearrange("p a b d -> p (a b d)").rearrange("p (m n) -> p m n", m=FC),
               qkT[:, :].rearrange("p a c b t -> p (a c b t)").rearrange("p (m n) -> p m n", m=FC)]
        acc = x_s

        block = ctx.enter_context(nc.Block())

        def heads(ap):
            return ap.rearrange("p (h d) -> p h d", h=H)

        @block.sync
        def _(sp):
            def load(name, dst, src):
                sp.dma_start(dst, src).then_inc(sem(name), 16)

            load("x_in", x_s[:, :, :], x)
            load("ctx_in", ctx_s[:, :, :], ctx_t)
            load("wk_in", wk_s, wk)
            load("wv_in", wv_s, wv)
            load("wq_in", wq_s, wq)
            load("wo_in", wo_s, wo)
            load("aq_in", aq_s, aq)
            load("ak_in", ak_s, ak)
            load("av_in", av_s, av)
            load("ao_in", ao_s, ao)
            for e in range(E):
                s = e % RING
                if e == 1:
                    sp.wait_ge(sem("out_psum1"), NB)
                elif e == 2:
                    sp.wait_ge(sem("pv_psum2"), 2 * NB)
                elif e == 3:
                    sp.wait_ge(sem("out_psum2"), NB)
                if e >= RING:
                    sp.wait_ge(sem("expert_psum"), NB * (e - RING + 1))
                load(f"w1_in{s}", w1_s[s], w1[e])
                load(f"w2_in{s}", w2_s[s], w2[e])
            for b in range(NB):
                sp.wait_ge(sem("result"), b + 1)
                sp.dma_start(out[:, b, :], acc[:, b, :]).then_inc(sem("stored"), 16)
            sp.wait_ge(sem("stored"), 16 * NB)

        @block.gpsimd
        def _(pool):
            pool.memset(ones_row[:, :], 1.0).then_inc(sem("ones_set"), 1)
            pool.memset(ident[:, :], 0.0).then_inc(sem("cleared"), 1)
            pool.memset(ident_h[:, :], 0.0).then_inc(sem("cleared"), 1)
            pool.memset(band[:, :, :], 0.0).then_inc(sem("cleared"), 1)
            pool.memset(eye2[:, :, :], 0.0).then_inc(sem("cleared"), 1)
            pool.memset(row_pick[:, :], 0.0).then_inc(sem("cleared"), 1)
            pool.memset(half_neg[:, :], -0.5).then_inc(sem("cleared"), 1)
            pool.memset(vv[:, :, :, HD:HD + 1], 1.0).then_inc(sem("ones_col"), 1)
            pool.wait_ge(sem("cleared"), 6)
            pool.affine_select(out=ident[:, :], in_=ident[:, :], compare_op=ALU.not_equal, fill=1.0, base=0,
                               pattern=[[-1, P]], channel_multiplier=1).then_inc(sem("ident_set"), 1)
            pool.affine_select(out=ident_h[:, :], in_=ident_h[:, :], compare_op=ALU.not_equal, fill=1.0, base=0,
                               pattern=[[-1, P]], channel_multiplier=1).then_inc(sem("ident_set"), 1)
            pool.affine_select(out=band[:, :, :], in_=band[:, :, :], compare_op=ALU.is_ge, fill=MASKED, base=0,
                               pattern=[[0, DC], [-1, P]], channel_multiplier=1).then_inc(sem("causal_set"), 1)
            pool.wait_ge(sem("causal_set"), 1)
            pool.affine_select(out=band[:, :, :], in_=band[:, :, :], compare_op=ALU.is_ge, fill=MASKED, base=WINDOW,
                               pattern=[[0, DC], [1, P]], channel_multiplier=-1).then_inc(sem("band_set"), 1)

            def root(n):
                pool.wait_ge(sem(f"var{n}"), NB)
                pool.tensor_scalar(veps[:, n, :], mv[:, n, :, 1], LN_EPS, None, ALU.add).then_inc(sem(f"veps{n}"), 1)
                pool.wait_ge(sem(f"veps{n}"), 1)
                pool.tensor_tensor(rstd[:, n, :], veps[:, n, :], half_neg[:, 0:1].to_broadcast((P, NB)),
                                   ALU.pow).then_inc(sem(f"rstd{n}"), 1)

            root(0)
            pool.affine_select(out=eye2[:, :, :], in_=eye2[:, :, :], compare_op=ALU.not_equal, fill=1.0, base=0,
                               pattern=[[0, NB], [-1, P]], channel_multiplier=1).then_inc(sem("eye_set"), 1)
            for g in range(3):
                if g == 0:
                    pool.wait_ge(sem("eye_set"), 1)
                else:
                    pool.wait_ge(sem("row_set"), g)
                rows = row_pick[g * H * C:(g + 1) * H * C, :]
                pool.affine_select(out=rows, in_=rows, compare_op=ALU.not_equal, fill=1.0, base=0,
                                   pattern=[[-1, H * C]], channel_multiplier=1).then_inc(sem("row_set"), 1)
            pool.wait_ge(sem("row_set"), 3)
            pool.iota(iota8[:, :], pattern=[[1, E]], base=0, channel_multiplier=0,
                      allow_small_or_imprecise_dtypes=True).then_inc(sem("iota_set"), 1)
            root(1)
            for h in range(H):
                pool.wait_ge(sem("decay_scan"), h + 1)
                pool.tensor_tensor(decay[0][:, h, :], decay[0][:, h, :], decay[1][:, h, :],
                                   ALU.add).then_inc(sem("decay_sum"), 1)
            root(2)
            root(3)

        @block.scalar
        def _(act):
            def load(name, dst, src):
                act.dma_start(dst, src).then_inc(sem(name), 16)

            load("bias_in", bias_s[:, :, :], biases)
            load("rope_in", rope_s[:, :, :], rope)
            load("wbeta_in", wbeta_s[:, :, :], wbeta)
            load("bbeta_in", bbeta_s[:, :], bbeta)
            load("gate_in", gate_s[:, :, :], gate_w)
            load("gateb_in", gateb_s[:, :], gate_b)
            load("b1_in", b1_s[:, :, :], b1)
            load("b2_in", b2_s[:, :], b2)
            load("norm_in", norm_s[:, :, :], norm_rows.partition_broadcast(P))

            def transposed(name, banks, dst):
                for b in range(NB):
                    act.wait_ge(sem(name + "_psum"), b + 1)
                    act.activation(dst[:, :, b, :], bank[banks[b]][:, :].rearrange("p (c t) -> p c t", c=DC),
                                   ACT.Copy).then_inc(sem(name + "_sb"), 1)

            def values(name, banks):
                for b in range(NB):
                    act.wait_ge(sem(name + "_psum"), b + 1)
                    act.activation(vv[:, b, :, 0:HD], heads(bank[banks[b]][:, :]), ACT.Copy).then_inc(
                        sem(name + "_sb"), 1)

            def feature(name, banks, dst):
                for b in range(NB):
                    act.wait_ge(sem(name + "_psum"), b + 1)
                    act.activation(dst[:, :, b, :], bank[banks[b]][:, :].rearrange("p (c t) -> p c t", c=DC),
                                   ACT.Relu, scale=-1.0).then_inc(sem(name + "_neg"), 1)
                    act.wait_ge(sem(name + "_neg"), b + 1)
                    act.activation(dst[:, :, b, :], dst[:, :, b, :], ACT.Exp, scale=-1.0).then_inc(
                        sem(name + "_exp"), 1)

            transposed("xnT", (6, 7), tT)
            act.wait_ge(sem("ones_col"), 1)
            values("v", (2, 3))
            transposed("kT", (6, 7), kT)
            transposed("qT", (0, 1), qT)
            for n in range(NB * G + 1):
                if n < NB * G:
                    b, j = divmod(n, G)
                    act.wait_ge(sem("shifted"), n + 1)
                    act.activation(probs[:, b, j], probs[:, b, j], ACT.Exp).then_inc(sem("prob"), 1)
                if n >= 1:
                    b, j = divmod(n - 1, G)
                    act.wait_ge(sem("probT_psum"), n)
                    act.activation(probsT[:, b, j].rearrange("p c k -> p (c k)"), bank[4 * b + j][:, :],
                                   ACT.Copy).then_inc(sem("probT_sb"), 1)
            transposed("mixT1", (1, 5), mixedT)
            transposed("x1nT", (0, 4), tT)
            act.wait_ge(sem("beta_logit"), 1)
            act.activation(beta_e[:, :, :], beta_r[:, :, :], ACT.Exp, scale=-1.0).then_inc(sem("beta_exp"), 1)
            act.wait_ge(sem("pv_psum1"), 4)
            values("v2", (2, 6))
            feature("q2T", (3, 7), qT)
            feature("k2T", (2, 6), kT)
            transposed("mixT2", (1, 5), mixedT)
            transposed("x2nT", (0, 4), tT)
            for b in range(NB):
                act.wait_ge(sem("lshift"), b + 1)
                act.activation(lge[:, b, :], lg[:, b, :], ACT.Exp).then_inc(sem("lexp"), 1)
            for e in range(E):
                act.wait_ge(sem("b1_in"), 16)
                for m in range(FC):
                    act.wait_ge(sem("hid_psum"), e * FC // 2 + m // 2 + 1)
                    if e >= 2 and m == 0:
                        act.wait_ge(sem("expert_psum"), NB * (e - 1))
                    ins = act.activation(hid[e % 2][:, m, :], bank[m // 2][:, (m % 2) * NB * P:(m % 2 + 1) * NB * P],
                                         ACT.Relu, bias=b1_s[:, e, m:m + 1])
                    if m % 2:
                        ins.then_inc(sem("hid_sb"), 1)

        @block.tensor
        def _(pe):
            def project(name, lhs, w, banks, bias=None, batches=range(NB)):
                for b in batches:
                    if bias is not None:
                        pe.matmul(bank[banks[b]][:, :], ones_row[:, :], bias_s[:, bias, :], start=True, stop=False)
                    for c in range(DC):
                        mm = pe.matmul(bank[banks[b]][:, :], lhs(c, b), w[:, c, :],
                                       start=(bias is None and c == 0), stop=(c == DC - 1))
                    mm.then_inc(sem(name), 1)

            def turn(name, ready, src, banks):
                for b in range(NB):
                    pe.wait_ge(sem(ready), b + 1)
                    for c in range(DC):
                        mm = pe.transpose(bank[banks[b]][:, c * P:(c + 1) * P], src[:, b, c * P:(c + 1) * P],
                                          ident[:, :])
                    mm.then_inc(sem(name + "_psum"), 1)

            def from_ctx(c, b):
                return ctx_s[:, c, b * P:(b + 1) * P]

            def from_tT(c, b):
                return tT[:, c, b, :]

            def from_mixedT(c, b):
                return mixedT[:, c, b, :]

            pe.wait_ge(sem("ones_set"), 1)
            pe.wait_ge(sem("bias_in"), 16)
            pe.wait_ge(sem("ctx_in"), 16)
            pe.wait_ge(sem("wk_in"), 16)
            project("k_psum", from_ctx, wk_s, (0, 1), 0)
            pe.wait_ge(sem("ident_set"), 2)
            turn("xnT", "xn0", xn, (6, 7))
            pe.wait_ge(sem("wv_in"), 16)
            project("v_psum", from_ctx, wv_s, (2, 3), 1)
            pe.wait_ge(sem("wq_in"), 16)
            pe.wait_ge(sem("xnT_sb"), NB)
            project("q_psum", from_tT, wq_s, (4, 5), 2)
            turn("kT", "k_rope", kr, (6, 7))
            turn("qT", "q_rope", qr, (0, 1))

            def head(ap, j, c, b):
                return ap[HD * j:HD * (j + 1), c, b, :]

            pe.wait_ge(sem("band_set"), 1)
            pe.wait_ge(sem("qT_sb"), NB)
            pe.wait_ge(sem("v_sb"), NB)
            pe.wait_ge(sem("kT_sb"), NB)
            for b in range(NB):
                for j in range(G):
                    pe.matmul(bank[4 * b + j][:, :], ident_h[:, :], band[:, :, :].rearrange("p c k -> p (c k)"),
                              start=True, stop=False, skip_group_check=True)
                for c in range(DC):
                    for j in range(G):
                        mm = pe.matmul(bank[4 * b + j][:, c * P:(c + 1) * P], head(qT, j, c, b), head(kT, j, c, b),
                                       start=False, stop=(c == DC - 1), skip_group_check=True)
                        if c == DC - 1:
                            mm.then_inc(sem("score_psum"), 1)

            def mix(name, ready, weights):
                for b in range(NB):
                    for j in range(G):
                        pe.wait_ge(sem(ready), b * G + j + 1)
                        for c in range(DC):
                            n = (j % 2) * DC + c
                            mm = pe.matmul(bank[4 * b + j // 2 * 2][:, n * (HD + 1):(n + 1) * (HD + 1)],
                                           weights(b, j, c), vv[:, b, G * c + j, :], start=True, stop=True,
                                           skip_group_check=True)
                        if j % 2:
                            mm.then_inc(sem(name), 1)

            for n in range(NB * G):
                b, j = divmod(n, G)
                pe.wait_ge(sem("prob"), n + 1)
                for c in range(DC):
                    mm = pe.transpose(bank[4 * b + j][:, c * P:(c + 1) * P], probs[:, b, j, c, :], ident[:, :])
                mm.then_inc(sem("probT_psum"), 1)
            mix("pv_psum1", "probT_sb", lambda b, j, c: probsT[:, b, j, c, :])
            turn("mixT1", "mixed1", mixed, (1, 5))
            pe.wait_ge(sem("wo_in"), 16)
            pe.wait_ge(sem("mixT1_sb"), NB)
            project("out_psum1", from_mixedT, wo_s, (3, 7), 3)

            turn("x1nT", "xn1", xn, (0, 4))
            pe.wait_ge(sem("wbeta_in"), 16)
            pe.wait_ge(sem("x1nT_sb"), NB)
            for c in range(DC):
                mm = pe.matmul(bank[1][0:H * C, 0:NB * P], wbeta_s[:, c, :], tT[:, c, :, :].rearrange(
                    "p b t -> p (b t)"), start=(c == 0), stop=(c == DC - 1))
            mm.then_inc(sem("beta_psum"), 1)
            pe.wait_ge(sem("aq_in"), 16)
            project("q2_psum", from_tT, aq_s, (2, 6))

            spread_bank = (1, 5, 0, 4)

            def spread(first, last):
                for h in range(first, last):
                    if h >= 4:
                        pe.wait_ge(sem("decay_scan"), h - 3)
                    for e in range(C):
                        mm = pe.matmul(bank[spread_bank[h % 4]][:, e * NB * P:(e + 1) * NB * P],
                                       row_pick[:, C * h + e:C * h + e + 1].to_broadcast((3 * H * C, P)), beta_p[:, :, :].rearrange("p b t -> p (b t)"),
                                       start=True, stop=True, skip_group_check=True)
                    mm.then_inc(sem("spread_psum"), 1)

            pe.wait_ge(sem("row_set"), 3)
            pe.wait_ge(sem("beta_parts"), 3)
            spread(0, 4)
            pe.wait_ge(sem("ak_in"), 16)
            project("k2_psum", from_tT, ak_s, (3, 7), batches=(0,))
            spread(4, 7)
            project("k2_psum", from_tT, ak_s, (3, 7), batches=(1,))
            spread(7, 10)
            pe.wait_ge(sem("av_in"), 16)
            for b in range(NB):
                pe.wait_ge(sem("q2_used"), b + 1)
                project("v2_psum", from_tT, av_s, (2, 6), batches=(b,))
                spread(10 + 3 * b, 13 + 3 * b)
            pe.wait_ge(sem("k2_used"), NB)
            turn("q2T", "q2_rope", qr, (3, 7))
            pe.wait_ge(sem("v2_sb"), NB)
            turn("k2T", "k2_rope", kr, (2, 6))
            pe.wait_ge(sem("q2T_sb"), NB)
            pe.wait_ge(sem("k2T_sb"), NB)
            pe.wait_ge(sem("decay_scan"), H)
            for b in range(NB):
                for c in range(DC):
                    for j in range(G):
                        mm = pe.matmul(bank[4 * b + j][:, c * P:(c + 1) * P], head(kT, j, c, b), head(qT, j, c, b),
                                       start=True, stop=True, skip_group_check=True)
                        if c == DC - 1:
                            mm.then_inc(sem("align_psum"), 1)
            mix("pv_psum2", "gated", lambda b, j, c: decay[0][:, G * c + j, b * P:(b + 1) * P])
            turn("mixT2", "mixed2", mixed, (1, 5))
            pe.wait_ge(sem("ao_in"), 16)
            pe.wait_ge(sem("mixT2_sb"), NB)
            project("out_psum2", from_mixedT, ao_s, (3, 7), 4)

            turn("x2nT", "xn3", xn, (0, 4))
            pe.wait_ge(sem("gate_in"), 16)
            pe.wait_ge(sem("gateb_in"), 16)
            pe.wait_ge(sem("x2nT_sb"), NB)
            for b in range(NB):
                pe.matmul(bank[1 + 4 * b][:, 0:E], ones_row[:, :], gateb_s[:, :], start=True, stop=False)
                for c in range(DC):
                    mm = pe.matmul(bank[1 + 4 * b][:, 0:E], tT[:, c, b, :], gate_s[:, c, :],
                                   start=False, stop=(c == DC - 1))
                mm.then_inc(sem("logit_psum"), 1)
            pe.wait_ge(sem("lshift"), NB)
            pe.wait_ge(sem("mixed2"), NB)

            def expert_in(e):
                s = e % RING
                pe.wait_ge(sem(f"w1_in{s}"), 16 * (e // RING + 1))
                for m in range(FC):
                    if e >= 1 and m % 2 == 0:
                        pe.wait_ge(sem("hid_sb"), (e - 1) * FC // 2 + m // 2 + 1)
                    for c in range(DC):
                        mm = pe.matmul(bank[m // 2][:, (m % 2) * NB * P:(m % 2 + 1) * NB * P],
                                       w1_s[s][:, c, m * P:(m + 1) * P],
                                       tT[:, c, :, :].rearrange("p b t -> p (b t)"),
                                       start=(c == 0), stop=(c == DC - 1), skip_group_check=True)
                    if m % 2:
                        mm.then_inc(sem("hid_psum"), 1)

            def expert_out(e):
                s = e % RING
                pe.wait_ge(sem(f"w2_in{s}"), 16 * (e // RING + 1))
                pe.wait_ge(sem("hid_sb"), (e + 1) * FC // 2)
                for b in range(NB):
                    if e >= 1:
                        pe.wait_ge(sem("expert_added"), NB * (e - 1) + b + 1)
                    for m in range(FC):
                        mm = pe.matmul(bank[4 + b][:, :], hid[e % 2][:, m, b * P:(b + 1) * P], w2_s[s][:, m, :],
                                       start=(m == 0), stop=(m == FC - 1))
                    mm.then_inc(sem("expert_psum"), 1)

            for e in range(E + 1):
                if e < E:
                    expert_in(e)
                if e >= 1:
                    expert_out(e - 1)
            pe.wait_ge(sem("gatep"), NB)
            for b in range(NB):
                pe.transpose(bank[6][0:E, b * P:(b + 1) * P], gatep[:, b, :], ident[:, :]).then_inc(
                    sem("gateT_psum"), 1)
            pe.wait_ge(sem("gateT_sb"), 1)
            pe.wait_ge(sem("b2_in"), 16)
            for b in range(NB):
                pe.wait_ge(sem("expert_added"), NB * (E - 1) + b + 1)
                pe.matmul(bank[4 + b][:, :], gatepT[:, b, :], b2_s[:, :], start=True, stop=True).then_inc(
                    sem("b2_psum"), 1)

        @block.vector
        def _(dve):
            def moments(n, src, ready):
                for b in range(NB):
                    for name, count in ready:
                        dve.wait_ge(sem(name), count(b))
                    dve.bn_stats(bstat[:, b, :], src[:, b, :]).then_inc(sem(f"stat{n}"), 1)
                    dve.wait_ge(sem(f"stat{n}"), b + 1)
                    dve.bn_aggr(mv[:, n, b, :], bstat[:, b, :]).then_inc(sem(f"var{n}"), 1)

            def normalise(n, src, dst):
                dve.wait_ge(sem(f"rstd{n}"), 1)
                dve.wait_ge(sem(f"var{n}"), NB)
                for b in range(NB):
                    dve.tensor_scalar(dst[:, b, :], src[:, b, :], mv[:, n, b, 0:1], rstd[:, n, b:b + 1],
                                      ALU.subtract, ALU.mult).then_inc(sem(f"xn{n}"), 1)

            def rotate(name, banks, tables, dst):
                for b in range(NB):
                    dve.wait_ge(sem(name + "_psum"), b + 1)
                    u = heads(bank[banks[b]][:, :])
                    ra, rb = heads(rope_a[:, b, :]), heads(rope_b[:, b, :])
                    cos = rope_s[:, tables:tables + 1, :].to_broadcast((P, H, HD))
                    sin = rope_s[:, tables + 1:tables + 2, :].to_broadcast((P, H, HD))
                    half = HD // 2
                    dve.tensor_tensor(ra, u, cos, ALU.mult).then_inc(sem(name + "_turned"), 1)
                    dve.tensor_tensor(rb[:, :, 0:half], u[:, :, half:HD], sin[:, :, 0:half], ALU.mult).then_inc(
                        sem(name + "_turned"), 1)
                    dve.tensor_tensor(rb[:, :, half:HD], u[:, :, 0:half], sin[:, :, half:HD], ALU.mult).then_inc(
                        sem(name + "_used"), 1)
                    dve.wait_ge(sem(name + "_turned"), 2 * b + 2)
                    dve.wait_ge(sem(name + "_used"), b + 1)
                    dve.tensor_tensor(dst[:, b, :], rope_a[:, b, :], rope_b[:, b, :], ALU.add).then_inc(
                        sem(name + "_rope"), 1)

            moments(0, x_s, [("x_in", lambda b: 16)])
            normalise(0, x_s, xn)
            dve.wait_ge(sem("rope_in"), 16)
            rotate("k", (0, 1), 2, kr)
            dve.wait_ge(sem("k_rope"), NB)
            rotate("q", (4, 5), 0, qr)
            for n in range(NB * G):
                b, j = divmod(n, G)
                dve.wait_ge(sem("score_psum"), n + 1)
                s = bank[4 * b + j][:, :].rearrange("p (c k) -> p c k", c=DC)
                dve.tensor_reduce(negmax[:, b, j, :], s, AX.X, ALU.max, negate=True).then_inc(sem("rowmax"), 1)
                dve.wait_ge(sem("rowmax"), n + 1)
                dve.tensor_tensor(probs[:, b, j], s, negmax[:, b, j, :, None].to_broadcast((P, DC, P)),
                                  ALU.add).then_inc(sem("shifted"), 1)

            def divide(name, psum, ready_eps):
                for b in range(NB):
                    for half in range(2):
                        dve.wait_ge(sem(psum), 2 * b + half + 1)
                        pv = bank[4 * b + 2 * half][:, 0:8 * (HD + 1)].rearrange("p (j c d) -> p j c d", j=2, c=DC)
                        dn = den[:, b, 8 * half:8 * half + 8].rearrange("p (j c) -> p j c", j=2)
                        if ready_eps:
                            dve.tensor_scalar(dn, pv[:, :, :, HD], DEN_EPS, None, ALU.add).then_inc(
                                sem(name + "_den"), 1)
                            dve.wait_ge(sem(name + "_den"), 2 * b + half + 1)
                            dve.reciprocal(dn, dn).then_inc(sem(name + "_rec"), 1)
                        else:
                            dve.reciprocal(dn, pv[:, :, :, HD]).then_inc(sem(name + "_rec"), 1)
                        dve.wait_ge(sem(name + "_rec"), 2 * b + half + 1)
                        o = mixed[:, b, :].rearrange("p (c j d) -> p j c d", c=DC, j=G)[:, 2 * half:2 * half + 2]
                        for j in range(2):
                            ins = dve.tensor_tensor(o[:, j], pv[:, j, :, 0:HD],
                                                    dn[:, j, :, None].to_broadcast((P, DC, HD)), ALU.mult)
                            if half == 1 and j == 1:
                                ins.then_inc(sem(name), 1)

            divide("mixed1", "pv_psum1", False)
            for b in range(NB):
                dve.wait_ge(sem("out_psum1"), b + 1)
                dve.tensor_tensor(x1[:, b, :], bank[3 + 4 * b][:, :], x_s[:, b, :], ALU.add).then_inc(sem("x1_sb"), 1)
            moments(1, x1, [("x1_sb", lambda b: b + 1)])
            normalise(1, x1, xn)

            dve.wait_ge(sem("bbeta_in"), 16)
            dve.wait_ge(sem("beta_psum"), 1)
            dve.tensor_scalar(beta_r[:, :, :].rearrange("p b t -> p (b t)"), bank[1][0:H * C, 0:NB * P],
                              bbeta_s[:, 0:1], -80.0, ALU.add, ALU.max).then_inc(sem("beta_logit"), 1)
            chain = sem("beta_step")
            dve.wait_ge(sem("beta_exp"), 1)
            dve.tensor_scalar(beta_e[:, :, :], beta_e[:, :, :], 1.0, None, ALU.add).then_inc(chain, 1)
            dve.wait_ge(chain, 1)
            dve.reciprocal(beta_r[:, :, :], beta_e[:, :, :]).then_inc(chain, 1)
            dve.wait_ge(chain, 2)
            dve.tensor_scalar(beta_r[:, :, :], beta_r[:, :, :], 0.001, 0.999, ALU.max, ALU.min).then_inc(chain, 1)
            dve.wait_ge(chain, 3)
            dve.memset(beta_r[:, :, 0:1], 0.0).then_inc(chain, 1)
            dve.wait_ge(chain, 4)
            hc = H * C
            dve.tensor_copy(beta_p[0:hc], beta_r[:, :, :]).then_inc(sem("beta_parts"), 1)
            dve.wait_ge(sem("beta_parts"), 1)
            dve.tensor_tensor(beta_e[:, :, :], beta_r[:, :, :], beta_p[0:hc], ALU.subtract).then_inc(chain, 1)
            dve.wait_ge(chain, 5)
            dve.tensor_copy(beta_p[hc:2 * hc], beta_e[:, :, :]).then_inc(sem("beta_parts"), 1)
            dve.wait_ge(sem("beta_parts"), 2)
            dve.tensor_copy(beta_r[:, :, :], beta_p[hc:2 * hc]).then_inc(chain, 1)
            dve.wait_ge(chain, 6)
            dve.tensor_tensor(beta_e[:, :, :], beta_e[:, :, :], beta_r[:, :, :], ALU.subtract).then_inc(chain, 1)
            dve.wait_ge(chain, 7)
            dve.tensor_copy(beta_p[2 * hc:3 * hc], beta_e[:, :, :]).then_inc(sem("beta_parts"), 1)

            def scans(first, last):
                for h in range(first, last):
                    dve.wait_ge(sem("spread_psum"), h + 1)
                    for e in range(C):
                        ins = dve.tensor_tensor_scan(decay[e][:, h, :],
                                                     bank[spread_bank[h % 4]][:, e * NB * P:(e + 1) * NB * P],
                                                     eye2[:, :, :].rearrange("p r t -> p (r t)"), 0.0,
                                                     ALU.mult, ALU.add)
                    ins.then_inc(sem("decay_scan"), 1)

            spread_bank = (1, 5, 0, 4)
            dve.wait_ge(sem("eye_set"), 1)
            dve.wait_ge(sem("probT_sb"), NB * G)
            dve.wait_ge(sem("pv_psum1"), 2 * NB)
            scans(0, 4)
            rotate("q2", (2, 6), 2, qr)
            scans(4, 8)
            rotate("k2", (3, 7), 2, kr)
            scans(8, H)

            def linear(name, banks, dst):
                for b in range(NB):
                    dve.wait_ge(sem(name + "_exp"), b + 1)
                    dve.scalar_tensor_tensor(out=dst[:, :, b, :],
                                             in0=bank[banks[b]][:, :].rearrange("p (c t) -> p c t", c=DC),
                                             scalar=0.0, in1=dst[:, :, b, :], op0=ALU.max, op1=ALU.add).then_inc(
                        sem(name + "_sb"), 1)

            linear("q2T", (3, 7), qT)
            linear("k2T", (2, 6), kT)
            for n in range(NB * G):
                b, j = divmod(n, G)
                dve.wait_ge(sem("align_psum"), n + 1)
                dve.wait_ge(sem("decay_sum"), H)
                d = decay[0][:, :, b * P:(b + 1) * P].rearrange("p (c j) t -> p j c t", j=G)[:, j]
                dve.tensor_tensor(d, bank[4 * b + j][:, :].rearrange("p (c t) -> p c t", c=DC), d,
                                  ALU.mult).then_inc(sem("gated"), 1)
            divide("mixed2", "pv_psum2", True)
            for b in range(NB):
                dve.wait_ge(sem("out_psum2"), b + 1)
                dve.tensor_tensor(rope_a[:, b, :], bank[3 + 4 * b][:, :], xn[:, b, :], ALU.add).then_inc(
                    sem("hh_sb"), 1)
            moments(2, rope_a, [("hh_sb", lambda b: b + 1)])
            normalise(2, rope_a, rope_b)
            dve.wait_ge(sem("norm_in"), 16)
            for b in range(NB):
                dve.wait_ge(sem("xn2"), b + 1)
                dve.tensor_tensor(rope_b[:, b, :], rope_b[:, b, :], norm_s[:, 0, :], ALU.mult).then_inc(
                    sem("x2_step"), 1)
                dve.wait_ge(sem("x2_step"), 3 * b + 1)
                dve.tensor_tensor(rope_b[:, b, :], rope_b[:, b, :], norm_s[:, 1, :], ALU.add).then_inc(
                    sem("x2_step"), 1)
                dve.wait_ge(sem("x2_step"), 3 * b + 2)
                dve.tensor_tensor(acc[:, b, :], rope_b[:, b, :], x1[:, b, :], ALU.add).then_inc(sem("x2_step"), 1)
                dve.wait_ge(sem("x2_step"), 3 * b + 3)
            moments(3, acc, [("x2_step", lambda b: 3 * b + 3)])
            normalise(3, acc, xn)

            for b in range(NB):
                dve.wait_ge(sem("logit_psum"), b + 1)
                pl = bank[1 + 4 * b][:, 0:E]
                dve.tensor_reduce(lmax[:, b:b + 1], pl, AX.X, ALU.max, negate=True).then_inc(sem("lmax"), 1)
                dve.wait_ge(sem("lmax"), b + 1)
                dve.tensor_scalar(lg[:, b, :], pl, lmax[:, b:b + 1], None, ALU.add).then_inc(sem("lshift"), 1)
            g = sem("gate_step")
            n = 0
            for b in range(NB):
                dve.wait_ge(sem("lexp"), b + 1)
                dve.tensor_reduce(lsum[:, b:b + 1], lge[:, b, :], AX.X, ALU.add).then_inc(g, 1)
                dve.wait_ge(g, n + 1)
                dve.reciprocal(lsum[:, b:b + 1], lsum[:, b:b + 1]).then_inc(g, 1)
                dve.wait_ge(g, n + 2)
                dve.tensor_scalar(lge[:, b, :], lge[:, b, :], lsum[:, b:b + 1], None, ALU.mult).then_inc(g, 1)
                dve.wait_ge(g, n + 3)
                dve.max(top8[:, b, :], lge[:, b, :]).then_inc(g, 1)
                dve.wait_ge(g, n + 4)
                dve.max_index(top_i[:, b, :], top8[:, b, :], lge[:, b, :]).then_inc(g, 1)
                dve.wait_ge(g, n + 5)
                dve.tensor_copy(top_f[:, b, :], top_i[:, b, :]).then_inc(g, 1)
                dve.wait_ge(g, n + 6)
                dve.wait_ge(sem("iota_set"), 1)
                for r in range(2):
                    dve.tensor_scalar(pick[:, r, b, :], iota8[:, :], top_f[:, b, r:r + 1], None,
                                      ALU.is_equal).then_inc(g, 1)
                dve.wait_ge(g, n + 8)
                dve.tensor_tensor(pick[:, 0, b, :], pick[:, 0, b, :], pick[:, 1, b, :], ALU.add).then_inc(g, 1)
                dve.wait_ge(g, n + 9)
                dve.tensor_tensor(gatep[:, b, :], lge[:, b, :], pick[:, 0, b, :], ALU.mult).then_inc(sem("gatep"), 1)
                n += 9
            dve.wait_ge(sem("gatep"), NB)
            for e in range(E):
                for b in range(NB):
                    dve.wait_ge(sem("expert_psum"), NB * e + b + 1)
                    if e >= 1:
                        dve.wait_ge(sem("expert_added"), NB * (e - 1) + b + 1)
                    dve.scalar_tensor_tensor(out=acc[:, b, :], in0=bank[4 + b][:, :], scalar=gatep[:, b, e:e + 1],
                                             in1=acc[:, b, :], op0=ALU.mult, op1=ALU.add).then_inc(
                        sem("expert_added"), 1)
            dve.wait_ge(sem("gateT_psum"), NB)
            dve.tensor_copy(gatepT[:, :, :].rearrange("p b t -> p (b t)"), bank[6][0:E, 0:NB * P]).then_inc(
                sem("gateT_sb"), 1)
            for b in range(NB):
                dve.wait_ge(sem("b2_psum"), b + 1)
                dve.wait_ge(sem("expert_added"), NB * (E - 1) + b + 1)
                dve.tensor_tensor(acc[:, b, :], bank[4 + b][:, :], acc[:, b, :], ALU.add).then_inc(sem("result"), 1)


def kernel(**inputs):
    import numpy as np
    import concourse.bacc as bacc
    from concourse.bass_utils import run_bass_kernel_spmd

    i = {k: np.asarray(v) for k, v in inputs.items()}

    def rows(w):
        return np.ascontiguousarray(w.reshape(-1, P, w.shape[-1]).transpose(1, 0, 2))

    half = HD // 2
    freq = (1.0 / 10000.0 ** (np.arange(half, dtype=np.float32) / half)).astype(np.float32)
    ang = np.arange(P, dtype=np.float32)[:, None] * freq[None, :]
    cos = np.concatenate([np.cos(ang), np.cos(ang)], 1)
    sin = np.concatenate([-np.sin(ang), np.sin(ang)], 1)
    scale = HD ** -0.5
    rope = np.stack([cos * scale, sin * scale, cos, sin], 1).astype(np.float32)

    arrays = {
        "x": np.ascontiguousarray(i["x"].transpose(1, 0, 2)),
        "ctx_t": rows(i["ctx_1024"][:, :P].transpose(2, 0, 1).reshape(D, NB * P)),
        "rope": rope,
        "wk": rows(i["L0_xattn_k_w"].T), "wv": rows(i["L0_xattn_v_w"].T),
        "wq": rows(i["L0_xattn_q_w"].T), "wo": rows(i["L0_xattn_o_w"].T),
        "aq": rows(i["L0_attn_Wq"]), "ak": rows(i["L0_attn_Wk"]),
        "av": rows(i["L0_attn_Wv"]), "ao": rows(i["L0_attn_Wo"]),
        "wbeta": rows(i["L0_attn_Wbeta"]),
        "bbeta": np.ascontiguousarray(i["L0_attn_bbeta"].reshape(H * C, 1)),
        "biases": np.stack([i["L0_xattn_k_b"], i["L0_xattn_v_b"], i["L0_xattn_q_b"], i["L0_xattn_o_b"],
                            i["L0_attn_bo"]])[None],
        "norm_rows": np.stack([i["L0_attn_ln_gamma"], i["L0_attn_ln_beta"]]),
        "gate_w": rows(i["L0_ffn_gate_w"].T),
        "gate_b": np.ascontiguousarray(i["L0_ffn_gate_b"].reshape(1, E)),
        "w1": np.ascontiguousarray(i["L0_ffn_w1"].reshape(E, DC, P, FF).transpose(0, 2, 1, 3)),
        "b1": np.ascontiguousarray(i["L0_ffn_b1"].reshape(E, FC, P).transpose(2, 0, 1)),
        "w2": np.ascontiguousarray(i["L0_ffn_w2"].reshape(E, FC, P, D).transpose(0, 2, 1, 3)),
        "b2": np.ascontiguousarray(i["L0_ffn_b2"]),
    }
    nc = bacc.Bacc("TRN2", target_bir_lowering=False, num_devices=1)
    args = [nc.dram_tensor(n, a.shape, mybir.dt.from_np(a.dtype), kind="ExternalInput").ap()
            for n, a in arrays.items()]
    out = nc.dram_tensor("out", (P, NB, D), F32, kind="ExternalOutput").ap()
    build(nc, *args, out)
    r = run_bass_kernel_spmd(nc, [arrays], core_ids=[0])
    return np.ascontiguousarray(r.results[0]["out"].transpose(1, 0, 2))
```

```python
from contextlib import ExitStack

import concourse.bass as bass
from concourse import mybir

F32 = mybir.dt.float32
BF16 = mybir.dt.bfloat16
F32R = mybir.dt.float32r
I32 = mybir.dt.int32
U32 = mybir.dt.uint32
ALU = mybir.AluOpType
ACT = mybir.ActivationFunctionType
AX = mybir.AxisListType

P = 128
NB = 2
D = 512
DC = D // P
H, HD = 16, 32
G = P // HD
WINDOW = 64
C = 2
E, FF = 8, 1024
FC = FF // P
RING = 3
SLOTS = P
FIRST_SLOT = 512
LN_EPS, DEN_EPS = 1e-5, 1e-6
MASKED = -1e30


def build(nc, x, ctx_t, rope, wk, wv, wq, wo, aq, ak, av, ao, wbeta, bbeta, biases, norm_rows,
          gate_w, gate_b, w1, b1, w2, b2, out):
    with ExitStack() as ctx:
        def sb(name, shape, dt=F32):
            return ctx.enter_context(nc.sbuf_tensor(name, shape, dt))

        sems = {}

        def sem(name):
            if name not in sems:
                sems[name] = ctx.enter_context(nc.semaphore(name))
            return sems[name]

        bank = [ctx.enter_context(nc.psum_tensor(f"bank{i}", [P, D], F32)) for i in range(8)]

        stage_w = [sb(f"stage_w{i}", [P, 8 * D]) for i in range(4)]
        proj = [stage_w[i // 2][:, (i % 2) * DC * D:(i % 2 + 1) * DC * D].rearrange("p (c n) -> p c n", c=DC)
                for i in range(8)]
        wk_s, wv_s, wq_s, wo_s, aq_s, ak_s, av_s, ao_s = proj
        x_s = sb("x_s", [P, NB, D])
        rope_s = sb("rope_s", [P, 4, HD])
        norm_s = sb("norm_s", [P, 2, D])
        wbeta_s = sb("wbeta_s", [P, DC, H * C])
        bbeta_s = sb("bbeta_s", [H * C, 1])
        gate_s = sb("gate_s", [P, DC, E])
        gateb_s = sb("gateb_s", [1, E])
        b1_s = sb("b1_s", [P, E, FC])
        b2_s = sb("b2_s", [E, D])

        ones_row = sb("ones_row", [1, P])
        ones_f = sb("ones_f", [P, HD])
        ident = sb("ident", [P, P])
        ident_h = sb("ident_h", [P, P], BF16)
        band = sb("band", [P, DC, P], BF16)
        eye4 = sb("eye4", [P, 4, P])
        row_pick = sb("row_pick", [3 * H * C, H * C], BF16)
        iota8 = sb("iota8", [P, E])
        slot_no = sb("slot_no", [P, SLOTS])
        before = sb("before", [P, P], BF16)
        ones_h = sb("ones_h", [P, P], BF16)
        zero_h = sb("zero_h", [P, 1], BF16)
        half_neg = sb("half_neg", [P, 1])

        bstat = sb("bstat", [P, NB, 6])
        mv = sb("mv", [P, 4, NB, 2])
        veps = sb("veps", [P, 4, NB])
        rstd = sb("rstd", [P, 4, NB])

        xn = sb("xn", [P, NB, D])
        tT = sb("tT", [P, DC, NB, P])
        x1 = sb("x1", [P, NB, D])

        negmax = sb("negmax", [P, NB, G, DC])
        beta_e = sb("beta_e", [H * C, NB, P])
        beta_r = sb("beta_r", [H * C, NB, P])
        beta_p = sb("beta_p", [3 * H * C, NB, P], BF16)
        lg = sb("lg", [P, NB, E])
        lge = sb("lge", [P, NB, E])
        lmax = sb("lmax", [P, NB])
        lsum = sb("lsum", [P, NB])
        top8 = sb("top8", [P, NB, 8])
        top_i = sb("top_i", [P, NB, 8], U32)
        top_f = sb("top_f", [P, NB, 8])
        pick = sb("pick", [P, 2, NB, E])
        gatep = sb("gatep", [P, NB, E])
        gatepT = sb("gatepT", [E, NB, P])
        early = ExitStack()

        def sb_early(name, shape, dt=F32):
            return early.enter_context(nc.sbuf_tensor(name, shape, dt))

        wide = [sb_early(f"wide{i}", [P, 8 * D]) for i in range(2)]
        ctx_s = sb_early("ctx_s", [P, DC, NB * P])
        rope_a = sb_early("rope_a", [P, NB, D])
        rope_b = sb_early("rope_b", [P, NB, D])
        qr = sb_early("qr", [P, NB, D])
        kr = sb_early("kr", [P, NB, D])
        qT = sb_early("qT", [P, DC, NB, P])
        kT = sb_early("kT", [P, DC, NB, P])
        vv = sb_early("vv", [P, NB, H, HD])
        row_sum = sb_early("row_sum", [P, NB, D])
        prob_sum = sb_early("prob_sum", [P, NB, G, DC])
        bias_s = sb_early("bias_s", [5, D])
        bias_part = sb_early("bias_part", [3 * HD, D], BF16)
        probs = [w[:, 0:4 * D].rearrange("p (j c k) -> p j c k", j=G, c=DC) for w in wide]
        probsT = [w[:, 4 * D:8 * D].rearrange("p (j c k) -> p j c k", j=G, c=DC) for w in wide]
        decay = [w[:, :].rearrange("p (h e t) -> p h e t", h=H, e=C) for w in wide]
        mixedT = qT
        acc = x_s

        early.close()
        x_part = sb("x_part", [P, 3, NB, D], BF16)
        x_rest = sb("x_rest", [P, NB, D])
        gate_part = sb("gate_part", [P, 3, NB, E], BF16)
        picked = sb("picked", [P, NB, E], BF16)
        place = sb("place", [P, 2, NB, E])
        overflow = sb("overflow", [P, 1], I32)
        most = sb("most", [P, 2])
        last_w = [sb(f"last_w{i}", [P, 8 * D]) for i in range(2)]
        w1_ring = [stage_w[0], stage_w[2], last_w[0]]
        w2_ring = [stage_w[1], stage_w[3], last_w[1]]
        w1_s = [w[:, :].rearrange("p (c n) -> p c n", c=DC) for w in w1_ring]
        w2_s = [w[:, :].rearrange("p (c n) -> p c n", c=FC) for w in w2_ring]
        onehot = sb("onehot", [P, 2, NB, SLOTS], BF16)
        spreadT = sb("spreadT", [P, 3, NB * P], F32R)
        slot_gate = sb("slot_gate", [P, 3])
        xg = sb("xg", [P, DC, SLOTS])
        hid = sb("hid", [P, FC, SLOTS])
        hid_hi = sb("hid_hi", [P, FC, SLOTS], F32R)
        hid_lo = sb("hid_lo", [P, FC, SLOTS], F32R)
        w2_hi = sb("w2_hi", [P, FC, D], F32R)
        w2_lo = sb("w2_lo", [P, FC, D], F32R)
        y_hi = sb("y_hi", [P, D], F32R)
        y_lo = sb("y_lo", [P, D], F32R)
        g_rest = sb("g_rest", [P, NB, E])

        block = ctx.enter_context(nc.Block())

        def norms(n, b):
            return NB * n + b + 1 if n < 2 else 2 * NB + 2 * b + n - 1

        def normed(n, b):
            return NB * min(n, 2) + b + 1

        def heads(ap):
            return ap.rearrange("p (h d) -> p h d", h=H)

        @block.sync
        def _(sp):
            def load(name, dst, src):
                sp.dma_start(dst, src).then_inc(sem(name), 16)

            for c in range(DC):
                load(f"k_in{c}", wk_s[:, c, :], wk[:, c, :])
                load(f"k_in{c}", ctx_s[:, c, :], ctx_t[:, c, :])
            load("x_in", x_s[:, :, :], x)
            load("wv_in", wv_s, wv)
            load("wq_in", wq_s, wq)
            load("wo_in", wo_s, wo)
            load("aq_in", aq_s, aq)
            load("ak_in", ak_s, ak)
            load("av_in", av_s, av)
            load("ao_in", ao_s, ao)

            def experts(turn):
                for e in range(E):
                    n = turn * E + e
                    s = n % RING
                    if n == 0:
                        sp.wait_ge(sem("out_psum1"), NB)
                    elif n == 1:
                        sp.wait_ge(sem("out_psum2"), NB)
                    elif n == 2:
                        sp.wait_ge(sem("mixed2"), DC * NB)
                        sp.wait_ge(sem("x2_step"), 3 * NB)
                    elif n >= RING:
                        sp.wait_ge(sem("hid_psum"), 2 * (n - RING + 1))
                    load(f"w1_in{s}", w1_s[s], w1[e])
                    if n >= RING:
                        sp.wait_ge(sem("w2_split"), 2 * (n - RING + 1))
                    load(f"w2_in{s}", w2_s[s], w2[e])

            experts(0)
            sp.wait_ge(sem("overflow_set"), 1)
            with sp.If(sp.value_load(overflow[0:1, 0:1], min_val=0, max_val=1) > 0):
                experts(1)
            for b in range(NB):
                sp.wait_ge(sem("result"), b + 1)
                sp.dma_start(out[:, b, :], acc[:, b, :]).then_inc(sem("stored"), 16)
            sp.wait_ge(sem("stored"), 16 * NB)

        @block.gpsimd
        def _(pool):
            pool.memset(bias_part[:, :], 0.0).then_inc(sem("bias_clear"), 1)
            pool.memset(row_pick[:, :], 0.0).then_inc(sem("cleared"), 1)
            pool.memset(ident[:, :], 0.0).then_inc(sem("cleared"), 1)
            for g in range(3):
                if g == 0:
                    pool.wait_ge(sem("cleared"), 2)
                else:
                    pool.wait_ge(sem("row_set"), g)
                rows = row_pick[g * H * C:(g + 1) * H * C, :]
                pool.affine_select(out=rows, in_=rows, compare_op=ALU.not_equal, fill=1.0, base=0,
                                   pattern=[[-1, H * C]], channel_multiplier=1).then_inc(sem("row_set"), 1)
            pool.wait_ge(sem("row_set"), 3)
            pool.affine_select(out=ident[:, :], in_=ident[:, :], compare_op=ALU.not_equal, fill=1.0, base=0,
                               pattern=[[-1, P]], channel_multiplier=1).then_inc(sem("ident_set"), 1)
            pool.memset(half_neg[:, :], -0.5).then_inc(sem("cleared"), 1)
            pool.memset(ident_h[:, :], 0.0).then_inc(sem("cleared"), 1)
            pool.memset(band[:, :, :], 0.0).then_inc(sem("cleared"), 1)
            pool.memset(eye4[:, :, :], 0.0).then_inc(sem("cleared"), 1)
            pool.memset(ones_h[:, :], 1.0).then_inc(sem("ones_set"), 1)
            pool.memset(ones_row[:, :], 1.0).then_inc(sem("ones_set"), 1)
            pool.memset(ones_f[:, :], 1.0).then_inc(sem("ones_set"), 1)
            pool.memset(zero_h[:, :], 0.0).then_inc(sem("ones_set"), 1)
            pool.wait_ge(sem("cleared"), 6)
            pool.affine_select(out=ident_h[:, :], in_=ident_h[:, :], compare_op=ALU.not_equal, fill=1.0, base=0,
                               pattern=[[-1, P]], channel_multiplier=1).then_inc(sem("ident_set"), 1)

            def root(n, b):
                pool.wait_ge(sem("var"), norms(n, b))
                pool.tensor_scalar(veps[:, n, b:b + 1], mv[:, n, b, 1:2], LN_EPS, None, ALU.add).then_inc(
                    sem("veps"), 1)
                pool.wait_ge(sem("veps"), norms(n, b))
                pool.tensor_tensor(rstd[:, n, b:b + 1], veps[:, n, b:b + 1], half_neg[:, 0:1], ALU.pow).then_inc(
                    sem("rstd"), 1)

            root(0, 0)
            root(0, 1)
            pool.affine_select(out=band[:, :, :], in_=band[:, :, :], compare_op=ALU.is_ge, fill=MASKED, base=0,
                               pattern=[[0, DC], [-1, P]], channel_multiplier=1).then_inc(sem("band_set"), 1)
            pool.wait_ge(sem("band_set"), 1)
            pool.affine_select(out=band[:, :, :], in_=band[:, :, :], compare_op=ALU.is_ge, fill=MASKED, base=WINDOW,
                               pattern=[[0, DC], [1, P]], channel_multiplier=-1).then_inc(sem("band_set"), 1)
            pool.affine_select(out=eye4[:, :, :], in_=eye4[:, :, :], compare_op=ALU.not_equal, fill=1.0, base=0,
                               pattern=[[0, 4], [-1, P]], channel_multiplier=1).then_inc(sem("eye_set"), 1)
            pool.iota(iota8[:, :], pattern=[[1, E]], base=0, channel_multiplier=0,
                      allow_small_or_imprecise_dtypes=True).then_inc(sem("iota_set"), 1)
            pool.iota(slot_no[:, :], pattern=[[1, SLOTS]], base=FIRST_SLOT, channel_multiplier=0,
                      allow_small_or_imprecise_dtypes=True).then_inc(sem("iota_set"), 1)
            pool.wait_ge(sem("ones_set"), 1)
            pool.affine_select(out=before[:, :], in_=ones_h[:, :], compare_op=ALU.is_gt, fill=0.0, base=0,
                               pattern=[[1, P]], channel_multiplier=-1).then_inc(sem("before_set"), 1)
            root(1, 0)
            root(1, 1)
            for b in range(NB):
                for i in range(H // 2):
                    pool.wait_ge(sem("decay_scan"), b * H // 2 + i + 1)
                    d = decay[b][:, 2 * i:2 * i + 2]
                    pool.tensor_tensor(d[:, :, 0, :], d[:, :, 0, :], d[:, :, 1, :], ALU.add).then_inc(
                        sem("decay_sum"), 1)
            for b in range(NB):
                root(2, b)
                root(3, b)
                for k in range(2):
                    pool.wait_ge(sem("x_part"), 3 * b + k + 1)
                    src = xn if k == 0 else x_rest
                    pool.tensor_tensor(x_rest[:, b, :], src[:, b, :], x_part[:, k, b, :], ALU.subtract).then_inc(
                        sem("x_rest"), 1)

        @block.scalar
        def _(act):
            def load(name, dst, src):
                act.dma_start(dst, src).then_inc(sem(name), 16)

            load("bias_in", bias_s[:, :], biases)
            load("rope_in", rope_s[:, :, :], rope)
            load("wbeta_in", wbeta_s[:, :, :], wbeta)
            load("bbeta_in", bbeta_s[:, :], bbeta)
            load("gate_in", gate_s[:, :, :], gate_w)
            load("gateb_in", gateb_s[:, :], gate_b)
            load("b1_in", b1_s[:, :, :], b1)
            load("b2_in", b2_s[:, :], b2)
            load("norm_in", norm_s[:, :, :], norm_rows.partition_broadcast(P))

            def split_bias():
                act.wait_ge(sem("bias_in"), 16)
                act.wait_ge(sem("bias_clear"), 1)
                for k in range(3):
                    if k:
                        act.wait_ge(sem("bias_rest"), k)
                    act.activation(bias_part[HD * k:HD * k + 5, :], bias_s[:, :], ACT.Copy).then_inc(
                        sem("bias_part"), 1)

            def transposed(name, b, i, dst):
                act.wait_ge(sem(name + "_psum"), b + 1)
                act.activation(dst[:, :, b, :], bank[4 * b + i][:, :].rearrange("p (c t) -> p c t", c=DC),
                               ACT.Copy).then_inc(sem(name + "_sb"), 1)

            def values(name, b, i):
                act.wait_ge(sem(name + "_psum"), b + 1)
                act.activation(vv[:, b, :, :], heads(bank[4 * b + i][:, :]), ACT.Copy).then_inc(sem(name + "_sb"), 1)

            def feature(name, b, i, dst):
                act.wait_ge(sem(name + "_psum"), b + 1)
                act.activation(dst[:, :, b, :], bank[4 * b + i][:, :].rearrange("p (c t) -> p c t", c=DC),
                               ACT.Relu, scale=-1.0).then_inc(sem(name + "_neg"), 1)
                act.wait_ge(sem(name + "_neg"), b + 1)
                act.activation(dst[:, :, b, :], dst[:, :, b, :], ACT.Exp, scale=-1.0).then_inc(
                    sem(name + "_exp"), 1)

            def exps(b, js):
                for j in js:
                    n = b * G + j
                    act.wait_ge(sem("rowmax"), n + 1)
                    for c in range(DC):
                        ins = act.activation(probs[b][:, j, c, :], bank[n][:, c * P:(c + 1) * P], ACT.Exp,
                                             bias=negmax[:, b, j, c:c + 1], accum_out=prob_sum[:, b, j, c:c + 1])
                    ins.then_inc(sem("exp"), 1)

            def probs_transposed(b):
                for j in range(G):
                    act.wait_ge(sem("probT_psum"), b * G + j + 1)
                    act.activation(probsT[b][:, j].rearrange("p c k -> p (c k)"), bank[4 * b + j][:, :],
                                   ACT.Copy).then_inc(sem("probT_sb"), 1)

            def beta_exp(b):
                act.wait_ge(sem("beta_logit"), b + 1)
                act.activation(beta_e[:, b, :], beta_r[:, b, :], ACT.Exp, scale=-1.0).then_inc(sem("beta_exp"), 1)

            def row_sums(b):
                act.wait_ge(sem("sums_psum"), b + 1)
                for half in range(2):
                    cols = slice(half * 2 * P, (half + 1) * 2 * P)
                    act.activation(row_sum[:, b, cols], bank[4 * b + 1][:, cols], ACT.Copy, bias=DEN_EPS).then_inc(
                        sem("row_sum"), 1)

            def gate_exp(b):
                act.wait_ge(sem("lshift"), b + 1)
                act.activation(lge[:, b, :], lg[:, b, :], ACT.Exp).then_inc(sem("lexp"), 1)

            def row_part(b, k):
                if k == 0:
                    act.wait_ge(sem("xn"), normed(3, b))
                else:
                    act.wait_ge(sem("x_rest"), 2 * b + k)
                src = xn if k == 0 else x_rest
                act.activation(x_part[:, k, b, :], src[:, b, :], ACT.Copy).then_inc(sem("x_part"), 1)

            split_bias()
            transposed("xnT", 0, 3, tT)
            transposed("xnT", 1, 3, tT)
            values("v", 0, 1)
            values("v", 1, 1)
            transposed("kT", 0, 3, kT)
            transposed("kT", 1, 3, kT)
            transposed("qT", 0, 0, qT)
            transposed("qT", 1, 0, qT)
            exps(0, range(G))
            exps(1, range(G))
            probs_transposed(1)
            transposed("x1nT", 0, 3, tT)
            beta_exp(0)
            values("v2", 0, 3)
            transposed("x1nT", 1, 3, tT)
            beta_exp(1)
            values("v2", 1, 3)
            feature("q2T", 0, 0, qT)
            feature("k2T", 0, 1, kT)
            row_sums(0)
            feature("q2T", 1, 0, qT)
            feature("k2T", 1, 1, kT)
            row_sums(1)
            for k in range(3):
                row_part(0, k)
            transposed("x2nT", 0, 3, tT)
            row_part(1, 0)
            gate_exp(0)
            transposed("x2nT", 1, 3, tT)
            row_part(1, 1)
            gate_exp(1)
            row_part(1, 2)

            def gathered(n):
                act.wait_ge(sem("gather_psum"), n + 1)
                act.activation(xg[:, :, :].rearrange("p c n -> p (c n)"), bank[2][:, :], ACT.Copy).then_inc(
                    sem("xg_sb"), 1)
                act.activation(slot_gate[:, n % 3:n % 3 + 1], bank[3][:, D - 1:D], ACT.Copy)
                act.activation(spreadT[:, n % 3, :], bank[3][:, 0:NB * P // 2].bitcast(BF16), ACT.Copy).then_inc(
                    sem("spreadT_sb"), 1)

            def experts(turn):
                for e in range(E):
                    n = turn * E + e
                    s = n % RING
                    if n == 0:
                        gathered(0)
                    act.wait_ge(sem(f"w2_in{s}"), 16 * (n // RING + 1))
                    for half in range(2):
                        if n >= 1:
                            act.wait_ge(sem(("w2_used", "y_psum")[half]), n)
                        rows = slice(4 * half, 4 * half + 4)
                        act.activation(w2_hi[:, rows, :], w2_s[s][:, rows, :], ACT.Copy).then_inc(sem("w2_hi"), 1)
                    for half in range(2):
                        act.wait_ge(sem("hid_psum"), 2 * n + half + 1)
                        rows = slice(4 * half, 4 * half + 4)
                        for m in range(4 * half, 4 * half + 4):
                            ins = act.activation(hid[:, m, :], bank[half][:, (m % 4) * P:(m % 4 + 1) * P], ACT.Relu,
                                                 bias=b1_s[:, e, m:m + 1])
                        ins.then_inc(sem("hid_sb"), 1)
                        act.wait_ge(sem("hid_sb"), 2 * n + half + 1)
                        act.activation(hid_hi[:, rows, :], hid[:, rows, :], ACT.Copy).then_inc(sem("hid_hi"), 1)
                    if turn == 0 and e < E - 1 or turn == 1 and e < E - 1:
                        gathered(n + 1)
                    act.wait_ge(sem("y_psum"), n + 1)
                    if n >= 1:
                        act.wait_ge(sem("returned"), n)
                    act.activation(y_hi[:, :], bank[6][:, :], ACT.Copy, scale=slot_gate[:, n % 3:n % 3 + 1]).then_inc(
                        sem("y_hi"), 1)

            act.wait_ge(sem("b1_in"), 16)
            experts(0)
            act.wait_ge(sem("overflow_set"), 1)
            with act.If(act.value_load(overflow[0:1, 0:1], min_val=0, max_val=1) > 0):
                gathered(E)
                experts(1)

        @block.tensor
        def _(pe):
            def project(name, b, i, lhs, w, ready, bias=None, between=None, inputs=None):
                o = bank[4 * b + i][:, :]
                if bias is not None:
                    add_bias(b, i, bias, start=True)
                for c in range(DC):
                    if b == 0 and c == 0:
                        pe.wait_ge(sem(ready), 16)
                    if inputs is not None:
                        pe.wait_ge(sem(inputs), inputs_count(inputs, b, c))
                    mm = pe.matmul(o, lhs(c, b), w[:, c, :], start=(bias is None and c == 0), stop=(c == DC - 1))
                    if c == DC - 1:
                        mm.then_inc(sem(name), 1)
                    if between is not None:
                        between(c)

            def inputs_count(name, b, c):
                return 2 * b + c // 2 + 1 if name == "mixed1" else DC * b + c + 1

            def add_bias(b, i, n, start):
                return pe.matmul(bank[4 * b + i][:, :], row_pick[:, n:n + 1].to_broadcast((3 * HD, P)),
                                 bias_part[:, :], start=start, stop=not start)

            def turn(name, b, i, src):
                for c in range(DC):
                    mm = pe.transpose(bank[4 * b + i][:, c * P:(c + 1) * P], src[:, b, c * P:(c + 1) * P],
                                      ident[:, :])
                mm.then_inc(sem(name + "_psum"), 1)

            def keep_clock(i, n, after=None):
                if after is not None:
                    pe.wait_ge(sem(after[0]), after[1])
                for _ in range(n):
                    pe.matmul(bank[i][:, :], ident_h[:, :], band[:, :, :].rearrange("p c k -> p (c k)"),
                              start=True, stop=True, skip_group_check=True)

            def from_ctx(c, b):
                return ctx_s[:, c, b * P:(b + 1) * P]

            def from_tT(c, b):
                return tT[:, c, b, :]

            def from_mixedT(c, b):
                return mixedT[:, c, b, :]

            def head(ap, j, c, b):
                return ap[HD * j:HD * (j + 1), c, b, :]

            def of_context(name, i, n, w):
                for c in range(DC):
                    if i == 0:
                        pe.wait_ge(sem(f"k_in{c}"), 32)
                    elif c == 0:
                        pe.wait_ge(sem("wv_in"), 16)
                    for b in range(NB):
                        pe.matmul(bank[4 * b + i][:, :], from_ctx(c, b), w[:, c, :], start=(c == 0), stop=False)
                if i == 0:
                    pe.wait_ge(sem("row_set"), 3)
                    pe.wait_ge(sem("bias_part"), 3)
                for b in range(NB):
                    add_bias(b, i, n, start=False).then_inc(sem(name), 1)

            def inputs_turned(b):
                pe.wait_ge(sem("xn"), normed(0, b))
                turn("xnT", b, 3, xn)

            def queries(b):
                pe.wait_ge(sem("xnT_sb"), b + 1)
                project("q_psum", b, 2, from_tT, wq_s, "wq_in", bias=2)

            def keys_turned(b):
                pe.wait_ge(sem("xnT_sb"), b + 1)
                pe.wait_ge(sem("k_rope"), b + 1)
                turn("kT", b, 3, kr)

            def queries_turned(b):
                pe.wait_ge(sem("q_rope"), b + 1)
                turn("qT", b, 0, qr)

            def mask(b, j):
                pe.wait_ge(sem(("qT_sb", "v_sb", "q_rope", "kT_sb")[j]), b + 1)
                pe.matmul(bank[4 * b + j][:, :], ident_h[:, :], band[:, :, :].rearrange("p c k -> p (c k)"),
                          start=True, stop=False, skip_group_check=True)

            def scores(b, js):
                if js[0] == 0:
                    mask(b, 0)
                for c in range(DC):
                    for j in js:
                        mm = pe.matmul(bank[4 * b + j][:, c * P:(c + 1) * P], head(qT, j, c, b), head(kT, j, c, b),
                                       start=False, stop=(c == DC - 1), skip_group_check=True)
                        if c == DC - 1:
                            mm.then_inc(sem("score_psum"), 1)

            def probs_turned(b, js):
                for j in js:
                    keep_clock(4 * b + j, 3 if b == 0 else 2, ("exp", b * G + j + 1))
                    pe.wait_ge(sem("prob"), b * G + j + 1)
                    for c in range(DC):
                        mm = pe.transpose(bank[4 * b + j][:, c * P:(c + 1) * P], probs[b][:, j, c, :], ident[:, :])
                    mm.then_inc(sem("probT_psum"), 1)

            def mix(b, name, ready, weights, rows=None):
                if rows is None:
                    pe.wait_ge(sem(ready), b * G + G)
                else:
                    for j in range(G):
                        pe.wait_ge(sem(ready), b * G + max(j + 1, 2))
                        mm = pe.matmul(bank[4 * b + 1][HD * j:HD * (j + 1), :], ones_f[:, :], rows(j),
                                       start=True, stop=True, skip_group_check=True)
                    mm.then_inc(sem("sums_psum"), 1)
                for c in range(DC):
                    for j in range(G):
                        mm = pe.matmul(bank[4 * b][HD * j:HD * (j + 1), c * P:(c + 1) * P], vv[:, b, G * c + j, :],
                                       weights(j, c), start=True, stop=True, skip_group_check=True)
                mm.then_inc(sem("pv" + name + "_psum"), 1)

            def mix1(b):
                mix(b, "1", "probT_sb", lambda j, c: probsT[b][:, j, c, :])

            def out1(b):
                project("out_psum1", b, 2, from_mixedT, wo_s, "wo_in", bias=3, inputs="mixed1")

            def inputs2_turned(b):
                pe.wait_ge(sem("xn"), normed(1, b))
                turn("x1nT", b, 3, xn)

            def beta_logits(b):
                pe.wait_ge(sem("wbeta_in"), 16)
                pe.wait_ge(sem("x1nT_sb"), b + 1)
                for c in range(DC):
                    mm = pe.matmul(bank[4 * b][0:H * C, 0:P], wbeta_s[:, c, :], tT[:, c, b, :],
                                   start=(c == 0), stop=(c == DC - 1))
                mm.then_inc(sem("beta_psum"), 1)

            def spread(b, i):
                n = b * H // 2 + i
                o = bank[4 * b + 3 * (i % 2)]
                if i == 0:
                    pe.wait_ge(sem("beta_parts"), 3 * (b + 1))
                elif i == 1:
                    pe.wait_ge(sem("v2_sb"), b + 1)
                else:
                    pe.wait_ge(sem("decay_scan"), n - 1)
                for k in range(2 * C):
                    mm = pe.matmul(o[:, k * P:(k + 1) * P],
                                   row_pick[:, 2 * C * i + k:2 * C * i + k + 1].to_broadcast((3 * H * C, P)),
                                   beta_p[:, b, :], start=True, stop=True, skip_group_check=True)
                mm.then_inc(sem("spread_psum"), 1)

            def spreads(b, steps):
                def between(c):
                    for i in steps.get(c, ()):
                        spread(b, i)
                return between

            def queries2(b):
                project("q2_psum", b, 1, from_tT, aq_s, "aq_in")

            def keys2(b, of=0, steps={}):
                project("k2_psum", b, 2, from_tT, ak_s, "ak_in", between=spreads(of, steps))

            def values2(b, of=0, steps={}):
                project("v2_psum", b, 3, from_tT, av_s, "av_in", between=spreads(of, steps))

            def queries2_turned(b):
                pe.wait_ge(sem("q2_rope"), b + 1)
                pe.wait_ge(sem("decay_scan"), (b + 1) * H // 2)
                turn("q2T", b, 0, qr)

            def keys2_turned(b):
                pe.wait_ge(sem("k2_rope"), b + 1)
                turn("k2T", b, 1, kr)

            def align(b):
                pe.wait_ge(sem("v2_sb"), b + 1)
                pe.wait_ge(sem("q2T_sb"), b + 1)
                pe.wait_ge(sem("k2T_sb"), b + 1)
                for c, j in [(c, j) for js in ((0, 1), (2, 3)) for c in range(DC) for j in js]:
                    mm = pe.matmul(bank[4 * b + j][:, c * P:(c + 1) * P], head(kT, j, c, b), head(qT, j, c, b),
                                   start=True, stop=True, skip_group_check=True)
                    if c == DC - 1:
                        mm.then_inc(sem("align_psum"), 1)

            def mix2(b):
                mix(b, "2", "gated", lambda j, c: decay[b][:, G * c + j, 0, :],
                    lambda j: decay[b][:, :, 0, :].rearrange("p (c j) t -> p j c t", j=G)[:, j])

            def out2(b):
                pe.wait_ge(sem("gated"), G * b + 3)
                project("out_psum2", b, 2, from_mixedT, ao_s, "ao_in", bias=4, inputs="mixed2")

            def inputs3_turned(b):
                pe.wait_ge(sem("xn"), normed(3, b))
                turn("x2nT", b, 3, xn)

            def logits(b):
                pe.wait_ge(sem("gate_in"), 16)
                pe.wait_ge(sem("ones_set"), 4)
                pe.wait_ge(sem("gateb_in"), 16)
                pe.wait_ge(sem("x2nT_sb"), b + 1)
                pe.matmul(bank[4 * b][:, 0:E], ones_row[:, :], gateb_s[:, :], start=True, stop=False)
                for c in range(DC):
                    mm = pe.matmul(bank[4 * b][:, 0:E], tT[:, c, b, :], gate_s[:, c, :],
                                   start=False, stop=(c == DC - 1))
                mm.then_inc(sem("logit_psum"), 1)

            of_context("k_psum", 0, 0, wk_s)
            pe.wait_ge(sem("ident_set"), 1)
            inputs_turned(0)
            inputs_turned(1)
            of_context("v_psum", 1, 1, wv_s)
            queries(0)
            keys_turned(0)
            keys_turned(1)
            queries(1)
            queries_turned(0)
            pe.wait_ge(sem("band_set"), 2)
            pe.wait_ge(sem("ident_set"), 2)
            keep_clock(1, 3, ("v_sb", 1))
            for j in range(1, G):
                mask(0, j)
            scores(0, (0, 1))
            scores(0, (2, 3))
            queries_turned(1)
            keep_clock(5, 3, ("v_sb", 2))
            for j in range(1, G):
                mask(1, j)
            scores(1, (0, 1))
            probs_turned(0, (0,))
            scores(1, (2, 3))
            probs_turned(0, (1, 2, 3))
            mix1(0)
            out1(0)
            probs_turned(1, range(G))
            mix1(1)
            inputs2_turned(0)
            beta_logits(0)
            out1(1)
            values2(0)
            queries2(0)
            inputs2_turned(1)
            beta_logits(1)
            keys2(0, 0, {0: (0,), 1: (1,), 2: (2,), 3: (3,)})
            values2(1, 0, {0: (4,), 1: (5,), 2: (6,), 3: (7,)})
            queries2(1)
            queries2_turned(0)
            keys2_turned(0)
            keys2(1, 1, {0: (0,), 1: (1,), 2: (2,), 3: (3,)})
            spread(1, 4)
            spread(1, 5)
            keep_clock(2, 4, ("k2_rope", 1))
            align(0)
            spread(1, 6)
            spread(1, 7)
            mix2(0)
            queries2_turned(1)
            keys2_turned(1)
            out2(0)
            align(1)
            mix2(1)
            keep_clock(6, 8, ("gated", 2 * G))
            out2(1)
            inputs3_turned(0)
            logits(0)
            keep_clock(6, 4, ("hh_sb", NB))
            keep_clock(6, 4, ("var", norms(2, 1)))
            keep_clock(6, 4, ("x2_step", 3 * NB))
            keep_clock(6, 4, ("var", norms(3, 1)))
            inputs3_turned(1)
            logits(1)
            pe.wait_ge(sem("before_set"), 1)
            pe.wait_ge(sem("picked"), NB)
            pe.matmul(bank[7][:, 0:E], before[:, :], picked[:, 0, :], start=True, stop=True, skip_group_check=True)
            pe.matmul(bank[7][:, E:2 * E], ones_h[:, :], picked[:, 0, :], start=True, stop=False,
                      skip_group_check=True)
            pe.matmul(bank[7][:, E:2 * E], before[:, :], picked[:, 1, :], start=False, stop=True,
                      skip_group_check=True)
            for b in range(NB):
                mm = pe.matmul(bank[7][:, 2 * E:3 * E], ones_h[:, :], picked[:, b, :], start=(b == 0),
                               stop=(b == NB - 1), skip_group_check=True)
            mm.then_inc(sem("rank_psum"), 1)

            def gather(n):
                pe.wait_ge(sem("onehot"), n + 1)
                if n == 0:
                    pe.wait_ge(sem("x_part"), 3 * NB)
                else:
                    pe.wait_ge(sem("spreadT_sb"), n)
                s = onehot[:, n % 2]
                e = n % E
                for c in range(DC):
                    for b in range(NB):
                        for k in range(3):
                            pe.matmul(bank[2][:, c * P:(c + 1) * P], x_part[:, k, b, c * P:(c + 1) * P], s[:, b, :],
                                      start=(b == 0 and k == 0), stop=(b == NB - 1 and k == 2),
                                      skip_group_check=True)
                for b in range(NB):
                    pe.transpose(bank[3][:, b * P // 2:(b + 1) * P // 2].bitcast(BF16), s[:, b, :], ident_h[:, :])
                if n == 0:
                    pe.wait_ge(sem("gate_parts"), 3)
                for b in range(NB):
                    for k in range(3):
                        mm = pe.matmul(bank[3][:, D - 1:D], s[:, b, :], gate_part[:, k, b, e:e + 1],
                                       start=(b == 0 and k == 0), stop=(b == NB - 1 and k == 2),
                                       skip_group_check=True)
                mm.then_inc(sem("gather_psum"), 1)

            def give_back(n):
                pe.wait_ge(sem("y_lo"), n + 1)
                for b in range(NB):
                    w = spreadT[:, n % 3, b * P:(b + 1) * P]
                    pe.matmul(bank[4 + b][:, :], w, y_hi[:, :], start=False, stop=False, skip_group_check=True)
                    mm = pe.matmul(bank[4 + b][:, :], w, y_lo[:, :], start=False, stop=False, skip_group_check=True)
                mm.then_inc(sem("returned"), 1)

            def experts(turn):
                for e in range(E):
                    n = turn * E + e
                    s = n % RING
                    pe.wait_ge(sem(f"w1_in{s}"), 16 * (n // RING + 1))
                    pe.wait_ge(sem("xg_sb"), n + 1)
                    for m in range(FC):
                        if n >= 1 and m % 4 == 0:
                            pe.wait_ge(sem("hid_sb"), 2 * (n - 1) + m // 4 + 1)
                        for c in range(DC):
                            mm = pe.matmul(bank[m // 4][:, (m % 4) * P:(m % 4 + 1) * P],
                                           w1_s[s][:, c, m * P:(m + 1) * P], xg[:, c, :],
                                           start=(c == 0), stop=(c == DC - 1), skip_group_check=True)
                        if m % 4 == 3:
                            mm.then_inc(sem("hid_psum"), 1)
                    if e < E - 1:
                        gather(n + 1)
                    if n >= 1:
                        give_back(n - 1)
                    for half in range(2):
                        pe.wait_ge(sem("hid_lo"), 2 * n + half + 1)
                        pe.wait_ge(sem("w2_split"), 2 * n + half + 1)
                        for m in range(4 * half, 4 * half + 4):
                            for k, (h, w) in enumerate(((hid_hi, w2_hi), (hid_hi, w2_lo), (hid_lo, w2_hi))):
                                mm = pe.matmul(bank[6][:, :], h[:, m, :], w[:, m, :], start=(m == 0 and k == 0),
                                               stop=(m == FC - 1 and k == 2), skip_group_check=True)
                        if half == 0:
                            mm.then_inc(sem("w2_used"), 1)
                    mm.then_inc(sem("y_psum"), 1)

            pe.wait_ge(sem("gatep"), NB)
            for b in range(NB):
                pe.transpose(bank[6][0:E, b * P:(b + 1) * P], gatep[:, b, :], ident[:, :]).then_inc(
                    sem("gateT_psum"), 1)
            gather(0)
            pe.wait_ge(sem("gateT_sb"), 1)
            pe.wait_ge(sem("b2_in"), 16)
            for b in range(NB):
                pe.matmul(bank[4 + b][:, :], gatepT[:, b, :], b2_s[:, :], start=True, stop=False,
                          skip_group_check=True)
            experts(0)
            pe.wait_ge(sem("overflow_set"), 1)
            with pe.If(pe.value_load(overflow[0:1, 0:1], min_val=0, max_val=1) > 0):
                gather(E)
                experts(1)
                give_back(2 * E - 1)
            with pe.If(pe.value_load(overflow[0:1, 0:1], min_val=0, max_val=1) < 1):
                give_back(E - 1)
            for b in range(NB):
                pe.matmul(bank[4 + b][:, 0:1], ident_h[:, :], zero_h[:, :], start=False, stop=True,
                          skip_group_check=True).then_inc(sem("sum_psum"), 1)

        @block.vector
        def _(dve):
            def moments(n, b, src):
                dve.bn_stats(bstat[:, b, :], src[:, b, :]).then_inc(sem("stat"), 1)
                dve.wait_ge(sem("stat"), norms(n, b))
                dve.bn_aggr(mv[:, n, b, :], bstat[:, b, :]).then_inc(sem("var"), 1)

            def normalise(n, b, src, dst):
                dve.wait_ge(sem("rstd"), norms(n, b))
                dve.tensor_scalar(dst[:, b, :], src[:, b, :], mv[:, n, b, 0:1], rstd[:, n, b:b + 1],
                                  ALU.subtract, ALU.mult).then_inc(sem("xn"), 1)

            def bias_rest():
                for k in range(2):
                    dve.wait_ge(sem("bias_part"), k + 1)
                    dve.tensor_tensor(bias_s[:, :], bias_s[:, :], bias_part[HD * k:HD * k + 5, :],
                                      ALU.subtract).then_inc(sem("bias_rest"), 1)

            turned = [0]

            def rotate(name, b, i, tables, dst, before=None):
                dve.wait_ge(sem(name + "_psum"), b + 1)
                u = heads(bank[4 * b + i][:, :])
                ra, rb = heads(rope_a[:, b, :]), heads(rope_b[:, b, :])
                cos = rope_s[:, tables:tables + 1, :].to_broadcast((P, H, HD))
                sin = rope_s[:, tables + 1:tables + 2, :].to_broadcast((P, H, HD))
                half = HD // 2
                if before:
                    dve.wait_ge(sem(before + "_rope"), b + 1)
                dve.tensor_tensor(ra, u, cos, ALU.mult).then_inc(sem("rope_term"), 1)
                dve.tensor_tensor(rb[:, :, 0:half], u[:, :, half:HD], sin[:, :, 0:half], ALU.mult).then_inc(
                    sem("rope_term"), 1)
                dve.tensor_tensor(rb[:, :, half:HD], u[:, :, 0:half], sin[:, :, half:HD], ALU.mult).then_inc(
                    sem("rope_term"), 1)
                turned[0] += 3
                dve.wait_ge(sem("rope_term"), turned[0])
                dve.tensor_tensor(dst[:, b, :], rope_a[:, b, :], rope_b[:, b, :], ALU.add).then_inc(
                    sem(name + "_rope"), 1)

            def row_maxima(b, js):
                for j in js:
                    n = b * G + j
                    dve.wait_ge(sem("score_psum"), n + 1)
                    dve.tensor_reduce(negmax[:, b, j, :], bank[n][:, :].rearrange("p (c k) -> p c k", c=DC), AX.X,
                                      ALU.max, negate=True).then_inc(sem("rowmax"), 1)

            def divide(b, js):
                for j in js:
                    n = b * G + j
                    dve.wait_ge(sem("exp"), n + 1)
                    dve.reciprocal(prob_sum[:, b, j, :], prob_sum[:, b, j, :]).then_inc(sem("prob_inverse"), 1)
                    dve.wait_ge(sem("prob_inverse"), n + 1)
                    dve.tensor_tensor(probs[b][:, j], probs[b][:, j],
                                      prob_sum[:, b, j, :, None].to_broadcast((P, DC, P)), ALU.mult).then_inc(
                        sem("prob"), 1)

            def probs_transposed(b, j):
                dve.wait_ge(sem("probT_psum"), b * G + j + 1)
                dve.tensor_copy(probsT[b][:, j].rearrange("p c k -> p (c k)"), bank[4 * b + j][:, :]).then_inc(
                    sem("probT_sb"), 1)

            def mixed1(b):
                dve.wait_ge(sem("pv1_psum"), b + 1)
                for half in range(2):
                    cs, cols = slice(2 * half, 2 * half + 2), slice(half * 2 * P, (half + 1) * 2 * P)
                    dve.tensor_copy(mixedT[:, cs, b, :],
                                    bank[4 * b][:, cols].rearrange("p (c t) -> p c t", c=2)).then_inc(
                        sem("mixed1"), 1)

            def divide2(b, *between):
                def inverse(c):
                    if c % 2 == 0:
                        dve.wait_ge(sem("row_sum"), 2 * b + c // 2 + 1)
                    part = row_sum[:, b, c * P:(c + 1) * P]
                    dve.reciprocal(part, part).then_inc(sem("inverse"), 1)

                inverse(0)
                inverse(1)
                if between:
                    between[0](*between[1:])
                dve.wait_ge(sem("pv2_psum"), b + 1)
                for c in range(DC):
                    dve.wait_ge(sem("inverse"), DC * b + c + 1)
                    dve.tensor_tensor(mixedT[:, c, b, :], bank[4 * b][:, c * P:(c + 1) * P],
                                      row_sum[:, b, c * P:(c + 1) * P], ALU.mult).then_inc(sem("mixed2"), 1)
                    if c + 2 < DC:
                        inverse(c + 2)

            def residual1(b):
                dve.wait_ge(sem("out_psum1"), b + 1)
                dve.tensor_tensor(x1[:, b, :], bank[4 * b + 2][:, :], x_s[:, b, :], ALU.add).then_inc(sem("x1_sb"), 1)
                dve.wait_ge(sem("x1_sb"), b + 1)
                moments(1, b, x1)

            def beta_logit(b):
                dve.wait_ge(sem("beta_psum"), b + 1)
                dve.wait_ge(sem("bbeta_in"), 16)
                dve.tensor_scalar(beta_r[:, b, :], bank[4 * b][0:H * C, 0:P], bbeta_s[:, 0:1], -80.0,
                                  ALU.add, ALU.max).then_inc(sem("beta_logit"), 1)

            def beta(b):
                chain, n = sem("beta_step"), 7 * b
                be, br = beta_e[:, b, :], beta_r[:, b, :]
                dve.wait_ge(sem("beta_exp"), b + 1)
                dve.tensor_scalar(be, be, 1.0, None, ALU.add).then_inc(chain, 1)
                dve.wait_ge(chain, n + 1)
                dve.reciprocal(br, be).then_inc(chain, 1)
                dve.wait_ge(chain, n + 2)
                dve.tensor_scalar(br, br, 0.001, 0.999, ALU.max, ALU.min).then_inc(chain, 1)
                dve.wait_ge(chain, n + 3)
                dve.memset(br[:, 0:1], 0.0).then_inc(chain, 1)
                dve.wait_ge(chain, n + 4)
                hc, part = H * C, sem("beta_parts")
                dve.tensor_copy(beta_p[0:hc, b, :], br).then_inc(part, 1)
                dve.wait_ge(part, 3 * b + 1)
                dve.tensor_tensor(be, br, beta_p[0:hc, b, :], ALU.subtract).then_inc(chain, 1)
                dve.wait_ge(chain, n + 5)
                dve.tensor_copy(beta_p[hc:2 * hc, b, :], be).then_inc(part, 1)
                dve.wait_ge(part, 3 * b + 2)
                dve.tensor_copy(br, beta_p[hc:2 * hc, b, :]).then_inc(chain, 1)
                dve.wait_ge(chain, n + 6)
                dve.tensor_tensor(be, be, br, ALU.subtract).then_inc(chain, 1)
                dve.wait_ge(chain, n + 7)
                dve.tensor_copy(beta_p[2 * hc:3 * hc, b, :], be).then_inc(part, 1)

            def scans(b, steps):
                if b == 0 and 0 in steps:
                    dve.wait_ge(sem("eye_set"), 1)
                for i in steps:
                    dve.wait_ge(sem("spread_psum"), b * H // 2 + i + 1)
                    dve.tensor_tensor_scan(decay[b][:, 2 * i:2 * i + 2].rearrange("p h e t -> p (h e t)"),
                                           bank[4 * b + 3 * (i % 2)][:, :], eye4[:, :, :].rearrange("p r t -> p (r t)"), 0.0,
                                           ALU.mult, ALU.add).then_inc(sem("decay_scan"), 1)

            def linear(name, b, i, dst):
                dve.wait_ge(sem(name + "_exp"), b + 1)
                dve.scalar_tensor_tensor(out=dst[:, :, b, :],
                                         in0=bank[4 * b + i][:, :].rearrange("p (c t) -> p c t", c=DC),
                                         scalar=0.0, in1=dst[:, :, b, :], op0=ALU.max, op1=ALU.add).then_inc(
                    sem(name + "_sb"), 1)

            def gate_scores(b):
                dve.wait_ge(sem("decay_sum"), (b + 1) * H // 2)
                for j in range(G):
                    dve.wait_ge(sem("align_psum"), b * G + j + 1)
                    d = decay[b][:, :, 0, :].rearrange("p (c j) t -> p j c t", j=G)[:, j]
                    dve.tensor_tensor(d, bank[4 * b + j][:, :].rearrange("p (c t) -> p c t", c=DC), d,
                                      ALU.mult).then_inc(sem("gated"), 1)

            def residual2(b):
                dve.wait_ge(sem("out_psum2"), b + 1)
                dve.tensor_tensor(rope_a[:, b, :], bank[4 * b + 2][:, :], xn[:, b, :], ALU.add).then_inc(
                    sem("hh_sb"), 1)
                dve.wait_ge(sem("hh_sb"), b + 1)
                moments(2, b, rope_a)

            def residual2_rest(b):
                if b == 0:
                    dve.wait_ge(sem("norm_in"), 16)
                dve.wait_ge(sem("var"), norms(2, b))
                dve.tensor_tensor(x1[:, b, :], x1[:, b, :], norm_s[:, 1, :], ALU.add).then_inc(sem("x2_step"), 1)
                dve.scalar_tensor_tensor(out=rope_b[:, b, :], in0=rope_a[:, b, :], scalar=mv[:, 2, b, 0:1],
                                         in1=norm_s[:, 0, :], op0=ALU.subtract, op1=ALU.mult).then_inc(
                    sem("x2_step"), 1)
                dve.wait_ge(sem("x2_step"), 3 * b + 2)
                dve.wait_ge(sem("rstd"), norms(2, b))
                dve.scalar_tensor_tensor(out=acc[:, b, :], in0=rope_b[:, b, :], scalar=rstd[:, 2, b:b + 1],
                                         in1=x1[:, b, :], op0=ALU.mult, op1=ALU.add).then_inc(sem("x2_step"), 1)
                dve.wait_ge(sem("x2_step"), 3 * b + 3)
                moments(3, b, acc)

            def route(b):
                dve.wait_ge(sem("logit_psum"), b + 1)
                pl = bank[4 * b][:, 0:E]
                dve.tensor_reduce(lmax[:, b:b + 1], pl, AX.X, ALU.max, negate=True).then_inc(sem("lmax"), 1)
                dve.wait_ge(sem("lmax"), b + 1)
                dve.tensor_scalar(lg[:, b, :], pl, lmax[:, b:b + 1], None, ALU.add).then_inc(sem("lshift"), 1)
                g, n = sem("gate_step"), 7 * b
                dve.wait_ge(sem("lexp"), b + 1)
                dve.tensor_reduce(lsum[:, b:b + 1], lge[:, b, :], AX.X, ALU.add).then_inc(g, 1)
                dve.wait_ge(g, n + 1)
                dve.reciprocal(lsum[:, b:b + 1], lsum[:, b:b + 1]).then_inc(g, 1)
                dve.wait_ge(g, n + 2)
                dve.tensor_scalar(lge[:, b, :], lge[:, b, :], lsum[:, b:b + 1], None, ALU.mult).then_inc(g, 1)
                dve.wait_ge(g, n + 3)
                dve.max(top8[:, b, :], lge[:, b, :]).then_inc(g, 1)
                dve.wait_ge(g, n + 4)
                dve.max_index(top_i[:, b, :], top8[:, b, :], lge[:, b, :]).then_inc(g, 1)
                dve.wait_ge(g, n + 5)
                dve.tensor_copy(top_f[:, b, :], top_i[:, b, :]).then_inc(g, 1)
                dve.wait_ge(g, n + 6)
                if b == 0:
                    dve.wait_ge(sem("iota_set"), 1)
                dve.tensor_scalar(pick[:, 1, b, :], iota8[:, :], top_f[:, b, 1:2], None, ALU.is_equal).then_inc(g, 1)
                dve.wait_ge(g, n + 7)
                dve.scalar_tensor_tensor(out=pick[:, 0, b, :], in0=iota8[:, :], scalar=top_f[:, b, 0:1],
                                         in1=pick[:, 1, b, :], op0=ALU.is_equal, op1=ALU.add).then_inc(
                    sem("pick"), 1)
                dve.wait_ge(sem("pick"), b + 1)
                dve.tensor_copy(picked[:, b, :], pick[:, 0, b, :]).then_inc(sem("picked"), 1)
                dve.tensor_tensor(gatep[:, b, :], lge[:, b, :], pick[:, 0, b, :], ALU.mult).then_inc(sem("gatep"), 1)

            bias_rest()
            dve.wait_ge(sem("x_in"), 16)
            moments(0, 0, x_s)
            moments(0, 1, x_s)
            normalise(0, 0, x_s, xn)
            normalise(0, 1, x_s, xn)
            dve.wait_ge(sem("rope_in"), 16)
            rotate("k", 0, 0, 2, kr)
            rotate("k", 1, 0, 2, kr)
            rotate("q", 0, 2, 0, qr, before="k")
            rotate("q", 1, 2, 0, qr, before="k")
            row_maxima(0, range(G))
            divide(0, (0, 1))
            row_maxima(1, (0,))
            probs_transposed(0, 0)
            row_maxima(1, (1,))
            divide(0, (2,))
            probs_transposed(0, 1)
            row_maxima(1, (2,))
            divide(0, (3,))
            probs_transposed(0, 2)
            row_maxima(1, (3,))
            probs_transposed(0, 3)
            mixed1(0)
            divide(1, range(G))
            residual1(0)
            normalise(1, 0, x1, xn)
            mixed1(1)
            beta_logit(0)
            beta(0)
            residual1(1)
            normalise(1, 1, x1, xn)
            rotate("q2", 0, 1, 2, qr, before="q")
            beta_logit(1)
            scans(0, (0, 1, 2, 3))
            rotate("k2", 0, 2, 2, kr, before="q2")
            scans(0, (4, 5))
            beta(1)
            scans(0, (6, 7))
            rotate("q2", 1, 1, 2, qr, before="q")
            linear("q2T", 0, 0, qT)
            linear("k2T", 0, 1, kT)
            scans(1, (0, 1, 2, 3))
            rotate("k2", 1, 2, 2, kr, before="q2")
            scans(1, (4, 5))
            gate_scores(0)
            scans(1, (6, 7))
            divide2(0)
            linear("q2T", 1, 0, qT)
            linear("k2T", 1, 1, kT)
            residual2(0)
            gate_scores(1)
            residual2_rest(0)
            divide2(1, normalise, 3, 0, acc, xn)
            residual2(1)
            residual2_rest(1)
            normalise(3, 1, acc, xn)
            route(0)
            route(1)

            dve.wait_ge(sem("rank_psum"), 1)
            dve.scalar_tensor_tensor(out=place[:, 0].rearrange("p b e -> p (b e)"), in0=bank[7][:, 0:NB * E],
                                     scalar=float(FIRST_SLOT), in1=pick[:, 0, :, :].rearrange("p b e -> p (b e)"),
                                     op0=ALU.add, op1=ALU.mult).then_inc(sem("place_step"), 1)
            dve.wait_ge(sem("place_step"), 1)
            dve.wait_ge(sem("iota_set"), 2)

            def one_hot(n):
                if n >= 2:
                    dve.wait_ge(sem("gather_psum"), n - 1)
                turn, e = divmod(n, E)
                for b in range(NB):
                    ins = dve.tensor_scalar(onehot[:, n % 2, b, :], slot_no[:, :], place[:, turn, b, e:e + 1], None,
                                            ALU.is_equal)
                ins.then_inc(sem("onehot"), 1)

            def experts(turn):
                for e in range(E):
                    n = turn * E + e
                    s = n % RING
                    for half in range(2):
                        dve.wait_ge(sem("w2_hi"), 2 * n + half + 1)
                        rows = slice(4 * half, 4 * half + 4)
                        dve.tensor_tensor(w2_lo[:, rows, :], w2_s[s][:, rows, :], w2_hi[:, rows, :].bitcast(F32),
                                          ALU.subtract).then_inc(sem("w2_split"), 1)
                    for half in range(2):
                        dve.wait_ge(sem("hid_hi"), 2 * n + half + 1)
                        rows = slice(4 * half, 4 * half + 4)
                        dve.tensor_tensor(hid_lo[:, rows, :], hid[:, rows, :], hid_hi[:, rows, :].bitcast(F32),
                                          ALU.subtract).then_inc(sem("hid_lo"), 1)
                    if e < E - 2:
                        one_hot(n + 2)
                    dve.wait_ge(sem("y_hi"), n + 1)
                    dve.scalar_tensor_tensor(out=y_lo[:, :], in0=bank[6][:, :], scalar=slot_gate[:, n % 3:n % 3 + 1],
                                             in1=y_hi[:, :].bitcast(F32), op0=ALU.mult,
                                             op1=ALU.subtract).then_inc(sem("y_lo"), 1)

            one_hot(0)
            for k in range(3):
                src = gatep if k == 0 else g_rest
                dve.tensor_copy(gate_part[:, k], src[:, :, :]).then_inc(sem("gate_parts"), 1)
                dve.wait_ge(sem("gate_parts"), k + 1)
                if k < 2:
                    dve.tensor_tensor(g_rest[:, :, :], src[:, :, :], gate_part[:, k], ALU.subtract).then_inc(
                        sem("g_rest"), 1)
                    dve.wait_ge(sem("g_rest"), k + 1)
            one_hot(1)
            dve.tensor_reduce(most[:, 0:1], bank[7][:, NB * E:(NB + 1) * E], AX.X, ALU.max).then_inc(
                sem("place_step"), 1)
            dve.tensor_scalar(place[:, 1], place[:, 0], -float(SLOTS), None, ALU.add).then_inc(sem("place_step"), 1)
            dve.wait_ge(sem("place_step"), 3)
            dve.tensor_scalar(most[:, 1:2], most[:, 0:1], float(SLOTS), None, ALU.is_gt).then_inc(sem("place_step"), 1)
            dve.wait_ge(sem("place_step"), 4)
            dve.wait_ge(sem("gateT_psum"), NB)
            dve.tensor_copy(gatepT[:, :, :].rearrange("p b t -> p (b t)"), bank[6][0:E, 0:NB * P]).then_inc(
                sem("gateT_sb"), 1)
            dve.tensor_copy(overflow[:, :], most[:, 1:2]).then_inc(sem("overflow_set"), 1)
            experts(0)
            dve.wait_ge(sem("overflow_set"), 1)
            with dve.If(dve.value_load(overflow[0:1, 0:1], min_val=0, max_val=1) > 0):
                one_hot(E)
                one_hot(E + 1)
                experts(1)
            for b in range(NB):
                dve.wait_ge(sem("sum_psum"), b + 1)
                dve.tensor_tensor(acc[:, b, :], bank[4 + b][:, :], acc[:, b, :], ALU.add).then_inc(sem("result"), 1)


def kernel(**inputs):
    import numpy as np
    import concourse.bacc as bacc
    from concourse.bass_utils import run_bass_kernel_spmd

    i = {k: np.asarray(v) for k, v in inputs.items()}

    def rows(w):
        return np.ascontiguousarray(w.reshape(-1, P, w.shape[-1]).transpose(1, 0, 2))

    half = HD // 2
    freq = (1.0 / 10000.0 ** (np.arange(half, dtype=np.float32) / half)).astype(np.float32)
    ang = np.arange(P, dtype=np.float32)[:, None] * freq[None, :]
    cos = np.concatenate([np.cos(ang), np.cos(ang)], 1)
    sin = np.concatenate([-np.sin(ang), np.sin(ang)], 1)
    scale = HD ** -0.5
    rope = np.stack([cos * scale, sin * scale, cos, sin], 1).astype(np.float32)

    arrays = {
        "x": np.ascontiguousarray(i["x"].transpose(1, 0, 2)),
        "ctx_t": rows(i["ctx_1024"][:, :P].transpose(2, 0, 1).reshape(D, NB * P)),
        "rope": rope,
        "wk": rows(i["L0_xattn_k_w"].T), "wv": rows(i["L0_xattn_v_w"].T),
        "wq": rows(i["L0_xattn_q_w"].T), "wo": rows(i["L0_xattn_o_w"].T),
        "aq": rows(i["L0_attn_Wq"]), "ak": rows(i["L0_attn_Wk"]),
        "av": rows(i["L0_attn_Wv"]), "ao": rows(i["L0_attn_Wo"]),
        "wbeta": rows(i["L0_attn_Wbeta"]),
        "bbeta": np.ascontiguousarray(i["L0_attn_bbeta"].reshape(H * C, 1)),
        "biases": np.stack([i["L0_xattn_k_b"], i["L0_xattn_v_b"], i["L0_xattn_q_b"], i["L0_xattn_o_b"],
                            i["L0_attn_bo"]]),
        "norm_rows": np.stack([i["L0_attn_ln_gamma"], i["L0_attn_ln_beta"]]),
        "gate_w": rows(i["L0_ffn_gate_w"].T),
        "gate_b": np.ascontiguousarray(i["L0_ffn_gate_b"].reshape(1, E)),
        "w1": np.ascontiguousarray(i["L0_ffn_w1"].reshape(E, DC, P, FF).transpose(0, 2, 1, 3)),
        "b1": np.ascontiguousarray(i["L0_ffn_b1"].reshape(E, FC, P).transpose(2, 0, 1)),
        "w2": np.ascontiguousarray(i["L0_ffn_w2"].reshape(E, FC, P, D).transpose(0, 2, 1, 3)),
        "b2": np.ascontiguousarray(i["L0_ffn_b2"]),
    }
    nc = bacc.Bacc("TRN2", target_bir_lowering=False, num_devices=1)
    args = [nc.dram_tensor(n, a.shape, mybir.dt.from_np(a.dtype), kind="ExternalInput").ap()
            for n, a in arrays.items()]
    out = nc.dram_tensor("out", (P, NB, D), F32, kind="ExternalOutput").ap()
    build(nc, *args, out)
    r = run_bass_kernel_spmd(nc, [arrays], core_ids=[0])
    return np.ascontiguousarray(r.results[0]["out"].transpose(1, 0, 2))
```

```python
from contextlib import ExitStack

import concourse.bass as bass
from concourse import mybir

F32 = mybir.dt.float32
BF16 = mybir.dt.bfloat16
F32R = mybir.dt.float32r
I32 = mybir.dt.int32
U32 = mybir.dt.uint32
ALU = mybir.AluOpType
ACT = mybir.ActivationFunctionType
AX = mybir.AxisListType

P = 128
NB = 2
D = 512
DC = D // P
H, HD = 16, 32
G = P // HD
WINDOW = 64
C = 2
E, FF = 8, 1024
FC = FF // P
RING = 3
SLOTS = P
FIRST_SLOT = 512
LN_EPS, DEN_EPS = 1e-5, 1e-6
MASKED = -1e30


def build(nc, x, ctx_t, rope, wk, wv, wq, wo, aq, ak, av, ao, wbeta, bbeta, biases, norm_rows,
          gate_w, gate_b, w1, b1, w2, b2, out):
    with ExitStack() as ctx:
        def sb(name, shape, dt=F32):
            return ctx.enter_context(nc.sbuf_tensor(name, shape, dt))

        sems = {}

        def sem(name):
            if name not in sems:
                sems[name] = ctx.enter_context(nc.semaphore(name))
            return sems[name]

        bank = [ctx.enter_context(nc.psum_tensor(f"bank{i}", [P, D], F32)) for i in range(8)]

        stage_w = [sb(f"stage_w{i}", [P, 8 * D]) for i in range(4)]
        proj = [stage_w[i // 2][:, (i % 2) * DC * D:(i % 2 + 1) * DC * D].rearrange("p (c n) -> p c n", c=DC)
                for i in range(8)]
        wk_s, wv_s, wq_s, wo_s, aq_s, ak_s, av_s, ao_s = proj
        x_s = sb("x_s", [P, NB, D])
        rope_s = sb("rope_s", [P, 4, HD])
        norm_s = sb("norm_s", [P, 2, D])
        wbeta_s = sb("wbeta_s", [P, DC, H * C])
        bbeta_s = sb("bbeta_s", [H * C, 1])
        gate_s = sb("gate_s", [P, DC, E])
        gateb_s = sb("gateb_s", [1, E])
        b1_s = sb("b1_s", [P, E, FC])
        b2_s = sb("b2_s", [E, D])

        ones_row = sb("ones_row", [1, P])
        ones_f = sb("ones_f", [P, HD])
        ident = sb("ident", [P, P])
        ident_h = sb("ident_h", [P, P], BF16)
        band = sb("band", [P, DC, P], BF16)
        eye4 = sb("eye4", [P, 4, P])
        row_pick = sb("row_pick", [3 * H * C, H * C], BF16)
        iota8 = sb("iota8", [P, E])
        slot_no = sb("slot_no", [P, SLOTS])
        before = sb("before", [P, P], BF16)
        ones_h = sb("ones_h", [P, P], BF16)
        zero_h = sb("zero_h", [P, 1], BF16)
        half_neg = sb("half_neg", [P, 1])

        bstat = sb("bstat", [P, NB, 6])
        mv = sb("mv", [P, 4, NB, 2])
        veps = sb("veps", [P, 4, NB])
        rstd = sb("rstd", [P, 4, NB])

        xn = sb("xn", [P, NB, D])
        tT = sb("tT", [P, DC, NB, P])
        x1 = sb("x1", [P, NB, D])

        negmax = sb("negmax", [P, NB, G, DC])
        beta_e = sb("beta_e", [H * C, NB, P])
        beta_r = sb("beta_r", [H * C, NB, P])
        beta_p = sb("beta_p", [3 * H * C, NB, P], BF16)
        lg = sb("lg", [P, NB, E])
        lge = sb("lge", [P, NB, E])
        lmax = sb("lmax", [P, NB])
        lsum = sb("lsum", [P, NB])
        top8 = sb("top8", [P, NB, 8])
        top_i = sb("top_i", [P, NB, 8], U32)
        top_f = sb("top_f", [P, NB, 8])
        pick = sb("pick", [P, 2, NB, E])
        gatep = sb("gatep", [P, NB, E])
        gatepT = sb("gatepT", [E, NB, P])
        early = ExitStack()

        def sb_early(name, shape, dt=F32):
            return early.enter_context(nc.sbuf_tensor(name, shape, dt))

        wide = [sb_early(f"wide{i}", [P, 8 * D]) for i in range(2)]
        ctx_s = sb_early("ctx_s", [P, DC, NB * P])
        rope_a = sb_early("rope_a", [P, NB, D])
        rope_b = sb_early("rope_b", [P, NB, D])
        qr = sb_early("qr", [P, NB, D])
        kr = sb_early("kr", [P, NB, D])
        qT = sb_early("qT", [P, DC, NB, P])
        kT = sb_early("kT", [P, DC, NB, P])
        vv = sb_early("vv", [P, NB, H, HD])
        row_sum = sb_early("row_sum", [P, NB, D])
        prob_sum = sb_early("prob_sum", [P, NB, G, DC])
        bias_s = sb_early("bias_s", [5, D])
        bias_part = sb_early("bias_part", [3 * HD, D], BF16)
        probs = [w[:, 0:4 * D].rearrange("p (j c k) -> p j c k", j=G, c=DC) for w in wide]
        probsT = [w[:, 4 * D:8 * D].rearrange("p (j c k) -> p j c k", j=G, c=DC) for w in wide]
        decay = [w[:, :].rearrange("p (h e t) -> p h e t", h=H, e=C) for w in wide]
        mixedT = qT
        acc = x_s

        early.close()
        x_hi = sb("x_hi", [P, NB, D], F32R)
        x_lo = sb("x_lo", [P, NB, D], F32R)
        gate_part = sb("gate_part", [P, 3, NB, E], BF16)
        picked = sb("picked", [P, NB, E], BF16)
        place = sb("place", [P, 2, NB, E])
        overflow = sb("overflow", [P, 1], I32)
        most = sb("most", [P, 2])
        last_w = [sb(f"last_w{i}", [P, 8 * D]) for i in range(2)]
        w1_ring = [stage_w[0], stage_w[2], last_w[0]]
        w2_ring = [stage_w[1], stage_w[3], last_w[1]]
        w1_s = [w[:, :].rearrange("p (c n) -> p c n", c=DC) for w in w1_ring]
        w2_s = [w[:, :].rearrange("p (c n) -> p c n", c=FC) for w in w2_ring]
        onehot_pair = sb("onehot_pair", [P, 2, NB, 2 * SLOTS], F32R)
        onehot = sb("onehot", [P, 2, NB, SLOTS], BF16)
        spreadT = sb("spreadT", [P, 3, NB * P], F32R)
        slot_gate = sb("slot_gate", [P, 3])
        xg = sb("xg", [P, DC, 2 * SLOTS])
        hid = sb("hid", [P, FC, SLOTS])
        hid_hi = sb("hid_hi", [P, FC, SLOTS], F32R)
        hid_lo = sb("hid_lo", [P, FC, SLOTS], F32R)
        w2_hi = sb("w2_hi", [P, FC, D], F32R)
        w2_lo = sb("w2_lo", [P, FC, D], F32R)
        y_hi = sb("y_hi", [P, D], F32R)
        y_lo = sb("y_lo", [P, D], F32R)
        g_rest = sb("g_rest", [P, NB, E])

        block = ctx.enter_context(nc.Block())

        def norms(n, b):
            return NB * n + b + 1 if n < 2 else 2 * NB + 2 * b + n - 1

        def normed(n, b):
            return NB * min(n, 2) + b + 1

        def heads(ap):
            return ap.rearrange("p (h d) -> p h d", h=H)

        @block.sync
        def _(sp):
            def load(name, dst, src):
                sp.dma_start(dst, src).then_inc(sem(name), 16)

            load("bias_in", bias_s[:, :], biases)
            for c in range(DC):
                load(f"k_in{c}", wk_s[:, c, :], wk[:, c, :])
                load(f"k_in{c}", ctx_s[:, c, :], ctx_t[:, c, :])
            load("x_in", x_s[:, :, :], x)
            load("wq_in", wq_s, wq)
            load("wv_in", wv_s, wv)
            load("wo_in", wo_s, wo)
            load("wbeta_in", wbeta_s[:, :, :], wbeta)
            load("bbeta_in", bbeta_s[:, :], bbeta)
            load("norm_in", norm_s[:, :, :], norm_rows.partition_broadcast(P))
            load("gate_in", gate_s[:, :, :], gate_w)
            load("gateb_in", gateb_s[:, :], gate_b)
            load("b1_in", b1_s[:, :, :], b1)
            load("b2_in", b2_s[:, :], b2)
            load("aq_in", aq_s, aq)
            load("ak_in", ak_s, ak)
            load("av_in", av_s, av)
            load("ao_in", ao_s, ao)

            def experts(turn):
                for e in range(E):
                    n = turn * E + e
                    s = n % RING
                    if n == 0:
                        sp.wait_ge(sem("out_psum1"), NB)
                    elif n == 1:
                        sp.wait_ge(sem("out_psum2"), NB)
                    elif n == 2:
                        sp.wait_ge(sem("mixed2"), DC * NB)
                        sp.wait_ge(sem("x2_step"), 2 * NB)
                    elif n >= RING:
                        sp.wait_ge(sem("hid_psum"), 2 * (n - RING + 1))
                    load(f"w1_in{s}", w1_s[s], w1[e])
                    if n >= RING:
                        sp.wait_ge(sem("w2_split"), 2 * (n - RING + 1))
                    load(f"w2_in{s}", w2_s[s], w2[e])

            experts(0)
            sp.wait_ge(sem("overflow_set"), 1)
            with sp.If(sp.value_load(overflow[0:1, 0:1], min_val=0, max_val=1) > 0):
                experts(1)
            for b in range(NB):
                sp.wait_ge(sem("result"), b + 1)
                sp.dma_start(out[:, b, :], acc[:, b, :]).then_inc(sem("stored"), 16)
            sp.wait_ge(sem("stored"), 16 * NB)

        @block.gpsimd
        def _(pool):
            pool.memset(bias_part[:, :], 0.0).then_inc(sem("bias_clear"), 1)
            pool.memset(row_pick[:, :], 0.0).then_inc(sem("cleared"), 1)
            pool.memset(ident[:, :], 0.0).then_inc(sem("cleared"), 1)
            for g in range(3):
                if g == 0:
                    pool.wait_ge(sem("cleared"), 2)
                else:
                    pool.wait_ge(sem("row_set"), g)
                rows = row_pick[g * H * C:(g + 1) * H * C, :]
                pool.affine_select(out=rows, in_=rows, compare_op=ALU.not_equal, fill=1.0, base=0,
                                   pattern=[[-1, H * C]], channel_multiplier=1).then_inc(sem("row_set"), 1)
            pool.wait_ge(sem("row_set"), 3)
            pool.affine_select(out=ident[:, :], in_=ident[:, :], compare_op=ALU.not_equal, fill=1.0, base=0,
                               pattern=[[-1, P]], channel_multiplier=1).then_inc(sem("ident_set"), 1)
            pool.memset(half_neg[:, :], -0.5).then_inc(sem("cleared"), 1)
            pool.memset(ident_h[:, :], 0.0).then_inc(sem("cleared"), 1)
            pool.memset(eye4[:, :, :], 0.0).then_inc(sem("cleared"), 1)
            pool.memset(ones_h[:, :], 1.0).then_inc(sem("ones_set"), 1)
            pool.memset(ones_row[:, :], 1.0).then_inc(sem("ones_set"), 1)
            pool.memset(ones_f[:, :], 1.0).then_inc(sem("ones_set"), 1)
            pool.memset(zero_h[:, :], 0.0).then_inc(sem("ones_set"), 1)
            pool.wait_ge(sem("cleared"), 5)
            pool.affine_select(out=ident_h[:, :], in_=ident_h[:, :], compare_op=ALU.not_equal, fill=1.0, base=0,
                               pattern=[[-1, P]], channel_multiplier=1).then_inc(sem("ident_set"), 1)

            def beta_parts(b):
                chain, n = sem("beta_rest"), 4 * b
                be, br = beta_e[:, b, :], beta_r[:, b, :]
                hc, part = H * C, sem("beta_parts")
                pool.wait_ge(sem("beta"), b + 1)
                pool.memset(br[:, 0:1], 0.0).then_inc(chain, 1)
                pool.wait_ge(chain, n + 1)
                pool.tensor_copy(beta_p[0:hc, b, :], br).then_inc(part, 1)
                pool.wait_ge(part, 3 * b + 1)
                pool.tensor_tensor(be, br, beta_p[0:hc, b, :], ALU.subtract).then_inc(chain, 1)
                pool.wait_ge(chain, n + 2)
                pool.tensor_copy(beta_p[hc:2 * hc, b, :], be).then_inc(part, 1)
                pool.wait_ge(part, 3 * b + 2)
                pool.tensor_copy(br, beta_p[hc:2 * hc, b, :]).then_inc(chain, 1)
                pool.wait_ge(chain, n + 3)
                pool.tensor_tensor(be, be, br, ALU.subtract).then_inc(chain, 1)
                pool.wait_ge(chain, n + 4)
                pool.tensor_copy(beta_p[2 * hc:3 * hc, b, :], be).then_inc(part, 1)
                pool.wait_ge(part, 3 * b + 3)

            def root(n, b):
                pool.wait_ge(sem("var"), norms(n, b))
                pool.tensor_scalar(veps[:, n, b:b + 1], mv[:, n, b, 1:2], LN_EPS, None, ALU.add).then_inc(
                    sem("veps"), 1)
                pool.wait_ge(sem("veps"), norms(n, b))
                pool.tensor_tensor(rstd[:, n, b:b + 1], veps[:, n, b:b + 1], half_neg[:, 0:1], ALU.pow).then_inc(
                    sem("rstd"), 1)

            root(0, 0)
            root(0, 1)
            pool.wait_ge(sem("band_clear"), 1)
            pool.wait_ge(sem("array_awake"), 1)
            pool.affine_select(out=band[:, :, :], in_=band[:, :, :], compare_op=ALU.is_ge, fill=MASKED, base=0,
                               pattern=[[0, DC], [-1, P]], channel_multiplier=1).then_inc(sem("band_set"), 1)
            pool.wait_ge(sem("band_set"), 1)
            pool.affine_select(out=band[:, :, :], in_=band[:, :, :], compare_op=ALU.is_ge, fill=MASKED, base=WINDOW,
                               pattern=[[0, DC], [1, P]], channel_multiplier=-1).then_inc(sem("band_set"), 1)
            pool.affine_select(out=eye4[:, :, :], in_=eye4[:, :, :], compare_op=ALU.not_equal, fill=1.0, base=0,
                               pattern=[[0, 4], [-1, P]], channel_multiplier=1).then_inc(sem("eye_set"), 1)
            pool.iota(iota8[:, :], pattern=[[1, E]], base=0, channel_multiplier=0,
                      allow_small_or_imprecise_dtypes=True).then_inc(sem("iota_set"), 1)
            pool.iota(slot_no[:, :], pattern=[[1, SLOTS]], base=FIRST_SLOT, channel_multiplier=0,
                      allow_small_or_imprecise_dtypes=True).then_inc(sem("iota_set"), 1)
            pool.wait_ge(sem("ones_set"), 1)
            pool.affine_select(out=before[:, :], in_=ones_h[:, :], compare_op=ALU.is_gt, fill=0.0, base=0,
                               pattern=[[1, P]], channel_multiplier=-1).then_inc(sem("before_set"), 1)
            pool.wait_ge(sem("norm_in"), 16)
            for b in range(NB):
                root(1, b)
                pool.wait_ge(sem("xn"), normed(1, b))
                pool.tensor_tensor(x1[:, b, :], x1[:, b, :], norm_s[:, 1, :], ALU.add).then_inc(sem("x1_beta"), 1)
                if b == 0:
                    beta_parts(0)

            def decay_sums(b, steps):
                for i in steps:
                    pool.wait_ge(sem("decay_scan"), b * H // 2 + i + 1)
                    d = decay[b][:, 2 * i:2 * i + 2]
                    pool.tensor_tensor(d[:, :, 0, :], d[:, :, 0, :], d[:, :, 1, :], ALU.add).then_inc(
                        sem("decay_sum"), 1)

            decay_sums(0, range(2))
            beta_parts(1)
            decay_sums(0, range(2, H // 2))
            decay_sums(1, range(H // 2))
            for b in range(NB):
                root(2, b)
                root(3, b)
                pool.wait_ge(sem("x_hi"), b + 1)
                pool.tensor_tensor(x_lo[:, b, :], xn[:, b, :], x_hi[:, b, :].bitcast(F32), ALU.subtract).then_inc(
                    sem("x_lo"), 1)

        @block.scalar
        def _(act):
            def load(name, dst, src):
                act.dma_start(dst, src).then_inc(sem(name), 16)

            load("rope_in", rope_s[:, :, :], rope)

            def split_bias():
                act.wait_ge(sem("bias_in"), 16)
                act.wait_ge(sem("bias_clear"), 1)
                for k in range(3):
                    if k:
                        act.wait_ge(sem("bias_rest"), k)
                    act.activation(bias_part[HD * k:HD * k + 5, :], bias_s[:, :], ACT.Copy).then_inc(
                        sem("bias_part"), 1)

            def transposed(name, b, i, dst):
                act.wait_ge(sem(name + "_psum"), b + 1)
                act.activation(dst[:, :, b, :], bank[4 * b + i][:, :].rearrange("p (c t) -> p c t", c=DC),
                               ACT.Copy).then_inc(sem(name + "_sb"), 1)

            def values(name, b, i, n):
                act.wait_ge(sem(name + "_psum"), n)
                act.activation(vv[:, b, :, :], heads(bank[i][:, :]), ACT.Copy).then_inc(sem(name + "_sb"), 1)

            def feature(name, b, i, dst):
                act.wait_ge(sem(name + "_psum"), b + 1)
                act.activation(dst[:, :, b, :], bank[4 * b + i][:, :].rearrange("p (c t) -> p c t", c=DC),
                               ACT.Relu, scale=-1.0).then_inc(sem(name + "_neg"), 1)
                act.wait_ge(sem(name + "_neg"), b + 1)
                act.activation(dst[:, :, b, :], dst[:, :, b, :], ACT.Exp, scale=-1.0).then_inc(
                    sem(name + "_exp"), 1)

            def exps(b, js):
                for j in js:
                    n = b * G + j
                    act.wait_ge(sem("rowmax"), n + 1)
                    for c in range(DC):
                        ins = act.activation(probs[b][:, j, c, :], bank[n][:, c * P:(c + 1) * P], ACT.Exp,
                                             bias=negmax[:, b, j, c:c + 1], accum_out=prob_sum[:, b, j, c:c + 1])
                    ins.then_inc(sem("exp"), 1)

            def probs_transposed(b):
                for j in range(G):
                    act.wait_ge(sem("probT_psum"), b * G + j + 1)
                    act.activation(probsT[b][:, j].rearrange("p c k -> p (c k)"), bank[4 * b + j][:, :],
                                   ACT.Copy).then_inc(sem("probT_sb"), 1)

            def beta_exp(b):
                act.wait_ge(sem("beta_logit"), b + 1)
                act.activation(beta_e[:, b, :], beta_r[:, b, :], ACT.Exp, scale=-1.0).then_inc(sem("beta_exp"), 1)

            def row_sums(b):
                act.wait_ge(sem("sums_psum"), b + 1)
                for half in range(2):
                    cols = slice(half * 2 * P, (half + 1) * 2 * P)
                    act.activation(row_sum[:, b, cols], bank[4 * b + 1][:, cols], ACT.Copy, bias=DEN_EPS).then_inc(
                        sem("row_sum"), 1)

            def gate_exp(b):
                act.wait_ge(sem("lshift"), b + 1)
                act.activation(lge[:, b, :], lg[:, b, :], ACT.Exp).then_inc(sem("lexp"), 1)

            def row_high(b):
                act.wait_ge(sem("xn"), normed(3, b))
                act.activation(x_hi[:, b, :], xn[:, b, :], ACT.Copy).then_inc(sem("x_hi"), 1)

            split_bias()
            transposed("xnT", 0, 3, tT)
            transposed("xnT", 1, 3, tT)
            transposed("kT", 0, 3, kT)
            transposed("kT", 1, 3, kT)
            transposed("qT", 0, 0, qT)
            exps(0, range(G))
            values("v", 1, 5, 1)
            values("v", 0, 7, 2)
            transposed("qT", 1, 0, qT)
            exps(1, range(G))
            probs_transposed(1)
            transposed("x1nT", 0, 3, tT)
            beta_exp(0)
            values("v2", 0, 3, 1)
            transposed("x1nT", 1, 3, tT)
            beta_exp(1)
            values("v2", 1, 7, 2)
            feature("q2T", 0, 0, qT)
            feature("k2T", 0, 1, kT)
            row_sums(0)
            feature("q2T", 1, 0, qT)
            feature("k2T", 1, 1, kT)
            row_sums(1)
            row_high(0)
            transposed("x2nT", 0, 3, tT)
            row_high(1)
            gate_exp(0)
            transposed("x2nT", 1, 3, tT)
            gate_exp(1)

            def gathered(n):
                if n % 2 == 0:
                    for half, i in enumerate((2, 7)):
                        act.wait_ge(sem("gather_psum"), n + half + 1)
                        ins = act.activation(xg[:, 2 * half:2 * half + 2, :].rearrange("p c n -> p (c n)"),
                                             bank[i][:, :], ACT.Copy)
                    ins.then_inc(sem("xg_sb"), 1)
                act.wait_ge(sem("back_psum"), n + 1)
                act.activation(slot_gate[:, n % 3:n % 3 + 1], bank[3][:, D - 1:D], ACT.Copy)
                act.activation(spreadT[:, n % 3, :], bank[3][:, 0:NB * P // 2].bitcast(BF16), ACT.Copy).then_inc(
                    sem("spreadT_sb"), 1)

            def experts(turn):
                for e in range(E):
                    n = turn * E + e
                    s = n % RING
                    if n == 0:
                        gathered(0)
                    act.wait_ge(sem(f"w2_in{s}"), 16 * (n // RING + 1))
                    for half in range(2):
                        if n >= 1:
                            act.wait_ge(sem(("w2_used", "y_psum")[half]), n)
                        rows = slice(4 * half, 4 * half + 4)
                        act.activation(w2_hi[:, rows, :], w2_s[s][:, rows, :], ACT.Copy).then_inc(sem("w2_hi"), 1)
                    for half in range(2):
                        act.wait_ge(sem("hid_psum"), 2 * n + half + 1)
                        rows = slice(4 * half, 4 * half + 4)
                        for m in range(4 * half, 4 * half + 4):
                            ins = act.activation(hid[:, m, :], bank[half][:, (m % 4) * P:(m % 4 + 1) * P], ACT.Relu,
                                                 bias=b1_s[:, e, m:m + 1])
                        ins.then_inc(sem("hid_sb"), 1)
                        act.wait_ge(sem("hid_sb"), 2 * n + half + 1)
                        act.activation(hid_hi[:, rows, :], hid[:, rows, :], ACT.Copy).then_inc(sem("hid_hi"), 1)
                    if e < E - 1:
                        gathered(n + 1)
                    act.wait_ge(sem("y_psum"), n + 1)
                    if n >= 1:
                        act.wait_ge(sem("returned"), n)
                    act.activation(y_hi[:, :], bank[6][:, :], ACT.Copy, scale=slot_gate[:, n % 3:n % 3 + 1]).then_inc(
                        sem("y_hi"), 1)

            act.wait_ge(sem("gateT_psum"), NB)
            act.activation(gatepT[:, :, :].rearrange("p b t -> p (b t)"), bank[6][0:E, 0:NB * P], ACT.Copy).then_inc(
                sem("gateT_sb"), 1)
            act.wait_ge(sem("b1_in"), 16)
            experts(0)
            act.wait_ge(sem("overflow_set"), 1)
            with act.If(act.value_load(overflow[0:1, 0:1], min_val=0, max_val=1) > 0):
                gathered(E)
                experts(1)

        @block.tensor
        def _(pe):
            def project(name, b, i, lhs, w, ready, bias=None, between=None, inputs=None):
                o = bank[4 * b + i][:, :]
                if bias is not None:
                    add_bias(b, i, bias, start=True)
                for c in range(DC):
                    if b == 0 and c == 0:
                        pe.wait_ge(sem(ready), 16)
                    if inputs is not None:
                        pe.wait_ge(sem(inputs), inputs_count(inputs, b, c))
                    mm = pe.matmul(o, lhs(c, b), w[:, c, :], start=(bias is None and c == 0), stop=(c == DC - 1))
                    if c == DC - 1:
                        mm.then_inc(sem(name), 1)
                    if between is not None:
                        between(c)

            def inputs_count(name, b, c):
                return 2 * b + c // 2 + 1 if name == "mixed1" else DC * b + c + 1

            def add_bias(b, i, n, start):
                return pe.matmul(bank[4 * b + i][:, :], row_pick[:, n:n + 1].to_broadcast((3 * HD, P)),
                                 bias_part[:, :], start=start, stop=not start)

            def turn(name, b, i, src):
                for c in range(DC):
                    mm = pe.transpose(bank[4 * b + i][:, c * P:(c + 1) * P], src[:, b, c * P:(c + 1) * P],
                                      ident[:, :])
                mm.then_inc(sem(name + "_psum"), 1)

            def keep_clock(i, n, after=None):
                if after is not None:
                    pe.wait_ge(sem(after[0]), after[1])
                for _ in range(n):
                    pe.matmul(bank[i][:, :], ident_h[:, :], band[:, :, :].rearrange("p c k -> p (c k)"),
                              start=True, stop=True, skip_group_check=True)

            def from_ctx(c, b):
                return ctx_s[:, c, b * P:(b + 1) * P]

            def from_tT(c, b):
                return tT[:, c, b, :]

            def from_mixedT(c, b):
                return mixedT[:, c, b, :]

            def head(ap, j, c, b):
                return ap[HD * j:HD * (j + 1), c, b, :]

            def keys():
                for c in range(DC):
                    pe.wait_ge(sem(f"k_in{c}"), 32)
                    for b in range(NB):
                        pe.matmul(bank[4 * b][:, :], from_ctx(c, b), wk_s[:, c, :], start=(c == 0), stop=False)
                pe.wait_ge(sem("row_set"), 3)
                pe.wait_ge(sem("bias_part"), 3)
                for b in range(NB):
                    add_bias(b, 0, 0, start=False).then_inc(sem("k_psum"), 1)

            def values(b):
                i = 5 if b == 1 else 7
                if b == 1:
                    pe.wait_ge(sem("wv_in"), 16)
                else:
                    pe.wait_ge(sem("kT_sb"), NB)
                add_bias(0, i, 1, start=True)
                for c in range(DC):
                    mm = pe.matmul(bank[i][:, :], from_ctx(c, b), wv_s[:, c, :], start=False, stop=(c == DC - 1))
                mm.then_inc(sem("v_psum"), 1)

            def inputs_turned(b):
                pe.wait_ge(sem("xn"), normed(0, b))
                turn("xnT", b, 3, xn)

            def queries(b):
                pe.wait_ge(sem("xnT_sb"), b + 1)
                project("q_psum", b, 2, from_tT, wq_s, "wq_in", bias=2)

            def keys_turned(b):
                pe.wait_ge(sem("xnT_sb"), b + 1)
                pe.wait_ge(sem("k_rope"), b + 1)
                turn("kT", b, 3, kr)

            def queries_turned(b):
                pe.wait_ge(sem("q_rope"), b + 1)
                turn("qT", b, 0, qr)

            def mask(b, j):
                if b == 1 and j % 2 == 1:
                    pe.wait_ge(sem("v_sb"), (j + 1) // 2)
                elif j != 1:
                    pe.wait_ge(sem(("qT_sb", None, "q_rope", "kT_sb")[j]), b + 1)
                pe.matmul(bank[4 * b + j][:, :], ident_h[:, :], band[:, :, :].rearrange("p c k -> p (c k)"),
                          start=True, stop=False, skip_group_check=True)

            def scores(b, js):
                if js[0] == 0:
                    mask(b, 0)
                for c in range(DC):
                    for j in js:
                        mm = pe.matmul(bank[4 * b + j][:, c * P:(c + 1) * P], head(qT, j, c, b), head(kT, j, c, b),
                                       start=False, stop=(c == DC - 1), skip_group_check=True)
                        if c == DC - 1:
                            mm.then_inc(sem("score_psum"), 1)

            def probs_turned(b, js, fill=2):
                for j in js:
                    keep_clock(4 * b + j, fill, ("exp", b * G + j + 1))
                    pe.wait_ge(sem("prob"), b * G + j + 1)
                    for c in range(DC):
                        mm = pe.transpose(bank[4 * b + j][:, c * P:(c + 1) * P], probs[b][:, j, c, :], ident[:, :])
                    mm.then_inc(sem("probT_psum"), 1)

            def mix(b, name, ready, weights, rows=None):
                if rows is None:
                    pe.wait_ge(sem(ready), b * G + G)
                else:
                    for j in range(G):
                        pe.wait_ge(sem(ready), b * G + max(j + 1, 2))
                        mm = pe.matmul(bank[4 * b + 1][HD * j:HD * (j + 1), :], ones_f[:, :], rows(j),
                                       start=True, stop=True, skip_group_check=True)
                    mm.then_inc(sem("sums_psum"), 1)
                for c in range(DC):
                    for j in range(G):
                        mm = pe.matmul(bank[4 * b][HD * j:HD * (j + 1), c * P:(c + 1) * P], vv[:, b, G * c + j, :],
                                       weights(j, c), start=True, stop=True, skip_group_check=True)
                mm.then_inc(sem("pv" + name + "_psum"), 1)

            def mix1(b):
                mix(b, "1", "probT_sb", lambda j, c: probsT[b][:, j, c, :])

            def out1(b):
                project("out_psum1", b, 2, from_mixedT, wo_s, "wo_in", bias=3, inputs="mixed1")

            def inputs2_turned(b):
                pe.wait_ge(sem("xn"), normed(1, b))
                turn("x1nT", b, 3, xn)

            def beta_logits(b):
                pe.wait_ge(sem("wbeta_in"), 16)
                pe.wait_ge(sem("x1nT_sb"), b + 1)
                for c in range(DC):
                    mm = pe.matmul(bank[4 * b][0:H * C, 0:P], wbeta_s[:, c, :], tT[:, c, b, :],
                                   start=(c == 0), stop=(c == DC - 1))
                mm.then_inc(sem("beta_psum"), 1)

            def spread(b, i):
                n = b * H // 2 + i
                o = bank[4 * b + 3 * (i % 2)]
                if i == 0:
                    pe.wait_ge(sem("beta_parts"), 3 * (b + 1))
                elif i == 1:
                    pe.wait_ge(sem("v2_sb"), b + 1)
                else:
                    pe.wait_ge(sem("decay_scan"), n - 1)
                for k in range(2 * C):
                    mm = pe.matmul(o[:, k * P:(k + 1) * P],
                                   row_pick[:, 2 * C * i + k:2 * C * i + k + 1].to_broadcast((3 * H * C, P)),
                                   beta_p[:, b, :], start=True, stop=True, skip_group_check=True)
                mm.then_inc(sem("spread_psum"), 1)

            def spreads(b, steps):
                def between(c):
                    for i in steps.get(c, ()):
                        spread(b, i)
                return between

            def queries2(b):
                project("q2_psum", b, 1, from_tT, aq_s, "aq_in")

            def keys2(b, of=0, steps={}):
                project("k2_psum", b, 2, from_tT, ak_s, "ak_in", between=spreads(of, steps))

            def values2(b, of=0, steps={}):
                project("v2_psum", b, 3, from_tT, av_s, "av_in", between=spreads(of, steps))

            def queries2_turned(b):
                pe.wait_ge(sem("q2_rope"), b + 1)
                pe.wait_ge(sem("decay_scan"), (b + 1) * H // 2)
                turn("q2T", b, 0, qr)

            def keys2_turned(b):
                pe.wait_ge(sem("k2_rope"), b + 1)
                turn("k2T", b, 1, kr)

            def align(b):
                pe.wait_ge(sem("v2_sb"), b + 1)
                pe.wait_ge(sem("q2T_sb"), b + 1)
                pe.wait_ge(sem("k2T_sb"), b + 1)
                for c, j in [(c, j) for js in ((0, 1), (2, 3)) for c in range(DC) for j in js]:
                    mm = pe.matmul(bank[4 * b + j][:, c * P:(c + 1) * P], head(kT, j, c, b), head(qT, j, c, b),
                                   start=True, stop=True, skip_group_check=True)
                    if c == DC - 1:
                        mm.then_inc(sem("align_psum"), 1)

            def mix2(b):
                mix(b, "2", "gated", lambda j, c: decay[b][:, G * c + j, 0, :],
                    lambda j: decay[b][:, :, 0, :].rearrange("p (c j) t -> p j c t", j=G)[:, j])

            def out2(b):
                def waiting(c):
                    if c == 0:
                        keep_clock(1, 1, ("row_sum", 2))
                    elif c < 3:
                        keep_clock(1, 1)

                pe.wait_ge(sem("gated"), G * b + 3)
                project("out_psum2", b, 2, from_mixedT, ao_s, "ao_in", bias=4, inputs="mixed2",
                        between=waiting if b == 0 else None)

            def inputs3_turned(b):
                pe.wait_ge(sem("xn"), normed(3, b))
                turn("x2nT", b, 3, xn)

            def logits(b):
                pe.wait_ge(sem("gate_in"), 16)
                pe.wait_ge(sem("ones_set"), 4)
                pe.wait_ge(sem("gateb_in"), 16)
                pe.wait_ge(sem("x2nT_sb"), b + 1)
                pe.matmul(bank[4 * b][:, 0:E], ones_row[:, :], gateb_s[:, :], start=True, stop=False)
                for c in range(DC):
                    mm = pe.matmul(bank[4 * b][:, 0:E], tT[:, c, b, :], gate_s[:, c, :],
                                   start=False, stop=(c == DC - 1))
                mm.then_inc(sem("logit_psum"), 1)

            pe.wait_ge(sem("band_clear"), 1)
            for _ in range(10):
                mm = pe.matmul(bank[7][:, :], band[:, 0, :], band[:, :, :].rearrange("p c k -> p (c k)"),
                               start=True, stop=True, skip_group_check=True)
            mm.then_inc(sem("array_awake"), 1)
            keys()
            pe.wait_ge(sem("ident_set"), 1)
            inputs_turned(0)
            inputs_turned(1)
            queries(0)
            keys_turned(0)
            keys_turned(1)
            queries(1)
            queries_turned(0)
            pe.wait_ge(sem("band_set"), 2)
            pe.wait_ge(sem("ident_set"), 2)
            keep_clock(1, 3)
            for j in range(1, G):
                mask(0, j)
            scores(0, (0, 1))
            scores(0, (2, 3))
            keep_clock(5, 4)
            values(1)
            probs_turned(0, (0, 1), fill=0)
            values(0)
            queries_turned(1)
            for j in range(1, G):
                mask(1, j)
            scores(1, (0, 1))
            probs_turned(0, (2, 3), fill=0)
            scores(1, (2, 3))
            mix1(0)
            out1(0)
            probs_turned(1, range(G))
            mix1(1)
            inputs2_turned(0)
            beta_logits(0)
            out1(1)
            values2(0)
            queries2(0)
            inputs2_turned(1)
            beta_logits(1)
            keys2(0, 0, {0: (0,), 1: (1,), 2: (2,), 3: (3,)})
            values2(1, 0, {0: (4,), 1: (5,), 2: (6,), 3: (7,)})
            queries2(1)
            queries2_turned(0)
            keys2_turned(0)
            keys2(1, 1, {0: (0,), 1: (1,), 2: (2,), 3: (3,)})
            spread(1, 4)
            spread(1, 5)
            keep_clock(2, 4, ("k2_rope", 1))
            align(0)
            spread(1, 6)
            spread(1, 7)
            mix2(0)
            queries2_turned(1)
            keys2_turned(1)
            out2(0)
            align(1)
            mix2(1)
            keep_clock(6, 3, ("gated", 2 * G))
            out2(1)
            inputs3_turned(0)
            logits(0)
            keep_clock(6, 3, ("hh_sb", NB))
            keep_clock(6, 3, ("var", norms(2, 1)))
            keep_clock(6, 3, ("x2_step", 2 * NB))
            keep_clock(6, 3, ("var", norms(3, 1)))
            inputs3_turned(1)
            logits(1)
            keep_clock(5, 6)
            keep_clock(5, 4, ("gate_step", 7 + 4))
            pe.wait_ge(sem("before_set"), 1)
            pe.wait_ge(sem("picked"), NB)
            pe.matmul(bank[7][:, 0:E], before[:, :], picked[:, 0, :], start=True, stop=True, skip_group_check=True)
            pe.matmul(bank[7][:, E:2 * E], ones_h[:, :], picked[:, 0, :], start=True, stop=False,
                      skip_group_check=True)
            pe.matmul(bank[7][:, E:2 * E], before[:, :], picked[:, 1, :], start=False, stop=True,
                      skip_group_check=True)
            for b in range(NB):
                mm = pe.matmul(bank[7][:, 2 * E:3 * E], ones_h[:, :], picked[:, b, :], start=(b == 0),
                               stop=(b == NB - 1), skip_group_check=True)
            mm.then_inc(sem("rank_psum"), 1)

            def gather(p):
                pe.wait_ge(sem("onehot_pair"), p + 1)
                if p == 0:
                    pe.wait_ge(sem("x_lo"), NB)
                for c in range(DC):
                    for b in range(NB):
                        for k, part in enumerate((x_hi, x_lo)):
                            mm = pe.matmul(bank[(2, 7)[c // 2]][:, (c % 2) * 2 * SLOTS:(c % 2 + 1) * 2 * SLOTS],
                                           part[:, b, c * P:(c + 1) * P], onehot_pair[:, p % 2, b, :],
                                           start=(b == 0 and k == 0), stop=(b == NB - 1 and k == 1),
                                           skip_group_check=True)
                    if c % 2 == 1:
                        mm.then_inc(sem("gather_psum"), 1)

            def way_back(n):
                pe.wait_ge(sem("onehot"), n + 1)
                if n >= 1:
                    pe.wait_ge(sem("spreadT_sb"), n)
                s = onehot[:, n % 2]
                e = n % E
                for b in range(NB):
                    pe.transpose(bank[3][:, b * P // 2:(b + 1) * P // 2].bitcast(BF16), s[:, b, :], ident_h[:, :])
                if n == 0:
                    pe.wait_ge(sem("gate_parts"), 3)
                for b in range(NB):
                    for k in range(3):
                        mm = pe.matmul(bank[3][:, D - 1:D], s[:, b, :], gate_part[:, k, b, e:e + 1],
                                       start=(b == 0 and k == 0), stop=(b == NB - 1 and k == 2),
                                       skip_group_check=True)
                mm.then_inc(sem("back_psum"), 1)

            def give_back(n):
                for half, y in (("y_hi", y_hi), ("y_lo", y_lo)):
                    pe.wait_ge(sem(half), n + 1)
                    for b in range(NB):
                        mm = pe.matmul(bank[4 + b][:, :], spreadT[:, n % 3, b * P:(b + 1) * P], y[:, :],
                                       start=False, stop=False, skip_group_check=True)
                mm.then_inc(sem("returned"), 1)

            def experts(turn):
                for e in range(E):
                    n = turn * E + e
                    s = n % RING
                    pe.wait_ge(sem(f"w1_in{s}"), 16 * (n // RING + 1))
                    pe.wait_ge(sem("xg_sb"), n // 2 + 1)
                    for m in range(FC):
                        if n >= 1 and m % 4 == 0:
                            pe.wait_ge(sem("hid_sb"), 2 * (n - 1) + m // 4 + 1)
                        for c in range(DC):
                            mm = pe.matmul(bank[m // 4][:, (m % 4) * P:(m % 4 + 1) * P],
                                           w1_s[s][:, c, m * P:(m + 1) * P],
                                           xg[:, c, n % 2 * SLOTS:(n % 2 + 1) * SLOTS],
                                           start=(c == 0), stop=(c == DC - 1), skip_group_check=True)
                        if m % 4 == 3:
                            mm.then_inc(sem("hid_psum"), 1)
                    if e < E - 1:
                        if n % 2 == 1:
                            gather((n + 1) // 2)
                        way_back(n + 1)
                    if n >= 1:
                        give_back(n - 1)
                    for half in range(2):
                        pe.wait_ge(sem("hid_lo"), 2 * n + half + 1)
                        pe.wait_ge(sem("w2_split"), 2 * n + half + 1)
                        for m in range(4 * half, 4 * half + 4):
                            for k, (h, w) in enumerate(((hid_hi, w2_hi), (hid_hi, w2_lo), (hid_lo, w2_hi))):
                                mm = pe.matmul(bank[6][:, :], h[:, m, :], w[:, m, :], start=(m == 0 and k == 0),
                                               stop=(m == FC - 1 and k == 2), skip_group_check=True)
                        if half == 0:
                            mm.then_inc(sem("w2_used"), 1)
                    mm.then_inc(sem("y_psum"), 1)

            pe.wait_ge(sem("gatep"), NB)
            for b in range(NB):
                pe.transpose(bank[6][0:E, b * P:(b + 1) * P], gatep[:, b, :], ident[:, :]).then_inc(
                    sem("gateT_psum"), 1)
            keep_clock(5, 2)
            gather(0)
            way_back(0)
            pe.wait_ge(sem("gateT_sb"), 1)
            pe.wait_ge(sem("b2_in"), 16)
            for b in range(NB):
                pe.matmul(bank[4 + b][:, :], gatepT[:, b, :], b2_s[:, :], start=True, stop=False,
                          skip_group_check=True)
            experts(0)
            pe.wait_ge(sem("overflow_set"), 1)
            with pe.If(pe.value_load(overflow[0:1, 0:1], min_val=0, max_val=1) > 0):
                gather(E // 2)
                way_back(E)
                experts(1)
                give_back(2 * E - 1)
            with pe.If(pe.value_load(overflow[0:1, 0:1], min_val=0, max_val=1) < 1):
                give_back(E - 1)
            for b in range(NB):
                pe.matmul(bank[4 + b][:, 0:1], ident_h[:, :], zero_h[:, :], start=False, stop=True,
                          skip_group_check=True).then_inc(sem("sum_psum"), 1)

        @block.vector
        def _(dve):
            def moments(n, b, src):
                if n == 3:
                    dve.wait_ge(sem("x2_step"), 2 * b + 2)
                dve.bn_stats(bstat[:, b, :], src[:, b, :]).then_inc(sem("stat"), 1)
                dve.wait_ge(sem("stat"), norms(n, b))
                dve.bn_aggr(mv[:, n, b, :], bstat[:, b, :]).then_inc(sem("var"), 1)

            def normalise(n, b, src, dst):
                dve.wait_ge(sem("rstd"), norms(n, b))
                dve.tensor_scalar(dst[:, b, :], src[:, b, :], mv[:, n, b, 0:1], rstd[:, n, b:b + 1],
                                  ALU.subtract, ALU.mult).then_inc(sem("xn"), 1)

            def bias_rest():
                for k in range(2):
                    dve.wait_ge(sem("bias_part"), k + 1)
                    dve.tensor_tensor(bias_s[:, :], bias_s[:, :], bias_part[HD * k:HD * k + 5, :],
                                      ALU.subtract).then_inc(sem("bias_rest"), 1)

            turned = [0]

            def rotate(name, b, i, tables, dst, before=None):
                dve.wait_ge(sem(name + "_psum"), b + 1)
                u = heads(bank[4 * b + i][:, :])
                ra, rb = heads(rope_a[:, b, :]), heads(rope_b[:, b, :])
                cos = rope_s[:, tables:tables + 1, :].to_broadcast((P, H, HD))
                sin = rope_s[:, tables + 1:tables + 2, :].to_broadcast((P, H, HD))
                half = HD // 2
                if before:
                    dve.wait_ge(sem(before + "_rope"), b + 1)
                dve.tensor_tensor(ra, u, cos, ALU.mult).then_inc(sem("rope_term"), 1)
                dve.tensor_tensor(rb[:, :, 0:half], u[:, :, half:HD], sin[:, :, 0:half], ALU.mult).then_inc(
                    sem("rope_term"), 1)
                dve.tensor_tensor(rb[:, :, half:HD], u[:, :, 0:half], sin[:, :, half:HD], ALU.mult).then_inc(
                    sem("rope_term"), 1)
                turned[0] += 3
                dve.wait_ge(sem("rope_term"), turned[0])
                dve.tensor_tensor(dst[:, b, :], rope_a[:, b, :], rope_b[:, b, :], ALU.add).then_inc(
                    sem(name + "_rope"), 1)

            def row_maxima(b, js):
                for j in js:
                    n = b * G + j
                    dve.wait_ge(sem("score_psum"), n + 1)
                    dve.tensor_reduce(negmax[:, b, j, :], bank[n][:, :].rearrange("p (c k) -> p c k", c=DC), AX.X,
                                      ALU.max, negate=True).then_inc(sem("rowmax"), 1)

            def divide(b, js):
                for j in js:
                    n = b * G + j
                    dve.wait_ge(sem("exp"), n + 1)
                    dve.reciprocal(prob_sum[:, b, j, :], prob_sum[:, b, j, :]).then_inc(sem("prob_inverse"), 1)
                    dve.wait_ge(sem("prob_inverse"), n + 1)
                    dve.tensor_tensor(probs[b][:, j], probs[b][:, j],
                                      prob_sum[:, b, j, :, None].to_broadcast((P, DC, P)), ALU.mult).then_inc(
                        sem("prob"), 1)

            def probs_transposed(b, j):
                dve.wait_ge(sem("probT_psum"), b * G + j + 1)
                dve.tensor_copy(probsT[b][:, j].rearrange("p c k -> p (c k)"), bank[4 * b + j][:, :]).then_inc(
                    sem("probT_sb"), 1)

            def mixed1(b):
                dve.wait_ge(sem("pv1_psum"), b + 1)
                for half in range(2):
                    cs, cols = slice(2 * half, 2 * half + 2), slice(half * 2 * P, (half + 1) * 2 * P)
                    dve.tensor_copy(mixedT[:, cs, b, :],
                                    bank[4 * b][:, cols].rearrange("p (c t) -> p c t", c=2)).then_inc(
                        sem("mixed1"), 1)

            def divide2(b, *between):
                def inverse(c):
                    if c % 2 == 0:
                        dve.wait_ge(sem("row_sum"), 2 * b + c // 2 + 1)
                    part = row_sum[:, b, c * P:(c + 1) * P]
                    dve.reciprocal(part, part).then_inc(sem("inverse"), 1)

                inverse(0)
                inverse(1)
                if between:
                    between[0](*between[1:])
                dve.wait_ge(sem("pv2_psum"), b + 1)
                for c in range(DC):
                    dve.wait_ge(sem("inverse"), DC * b + c + 1)
                    dve.tensor_tensor(mixedT[:, c, b, :], bank[4 * b][:, c * P:(c + 1) * P],
                                      row_sum[:, b, c * P:(c + 1) * P], ALU.mult).then_inc(sem("mixed2"), 1)
                    if c + 2 < DC:
                        inverse(c + 2)

            def residual1(b):
                dve.wait_ge(sem("out_psum1"), b + 1)
                dve.tensor_tensor(x1[:, b, :], bank[4 * b + 2][:, :], x_s[:, b, :], ALU.add).then_inc(sem("x1_sb"), 1)
                dve.wait_ge(sem("x1_sb"), b + 1)
                moments(1, b, x1)

            def beta_logit(b):
                dve.wait_ge(sem("beta_psum"), b + 1)
                dve.wait_ge(sem("bbeta_in"), 16)
                dve.tensor_scalar(beta_r[:, b, :], bank[4 * b][0:H * C, 0:P], bbeta_s[:, 0:1], -80.0,
                                  ALU.add, ALU.max).then_inc(sem("beta_logit"), 1)

            def beta(b):
                chain, n = sem("beta_step"), 2 * b
                be, br = beta_e[:, b, :], beta_r[:, b, :]
                dve.wait_ge(sem("beta_exp"), b + 1)
                dve.tensor_scalar(be, be, 1.0, None, ALU.add).then_inc(chain, 1)
                dve.wait_ge(chain, n + 1)
                dve.reciprocal(br, be).then_inc(chain, 1)
                dve.wait_ge(chain, n + 2)
                dve.tensor_scalar(br, br, 0.001, 0.999, ALU.max, ALU.min).then_inc(sem("beta"), 1)

            def scans(b, steps):
                if b == 0 and 0 in steps:
                    dve.wait_ge(sem("eye_set"), 1)
                for i in steps:
                    dve.wait_ge(sem("spread_psum"), b * H // 2 + i + 1)
                    dve.tensor_tensor_scan(decay[b][:, 2 * i:2 * i + 2].rearrange("p h e t -> p (h e t)"),
                                           bank[4 * b + 3 * (i % 2)][:, :], eye4[:, :, :].rearrange("p r t -> p (r t)"), 0.0,
                                           ALU.mult, ALU.add).then_inc(sem("decay_scan"), 1)

            def linear(name, b, i, dst):
                dve.wait_ge(sem(name + "_exp"), b + 1)
                dve.scalar_tensor_tensor(out=dst[:, :, b, :],
                                         in0=bank[4 * b + i][:, :].rearrange("p (c t) -> p c t", c=DC),
                                         scalar=0.0, in1=dst[:, :, b, :], op0=ALU.max, op1=ALU.add).then_inc(
                    sem(name + "_sb"), 1)

            def gate_scores(b):
                dve.wait_ge(sem("decay_sum"), (b + 1) * H // 2)
                for j in range(G):
                    dve.wait_ge(sem("align_psum"), b * G + j + 1)
                    d = decay[b][:, :, 0, :].rearrange("p (c j) t -> p j c t", j=G)[:, j]
                    dve.tensor_tensor(d, bank[4 * b + j][:, :].rearrange("p (c t) -> p c t", c=DC), d,
                                      ALU.mult).then_inc(sem("gated"), 1)

            def residual2(b):
                dve.wait_ge(sem("out_psum2"), b + 1)
                dve.tensor_tensor(rope_a[:, b, :], bank[4 * b + 2][:, :], xn[:, b, :], ALU.add).then_inc(
                    sem("hh_sb"), 1)
                dve.wait_ge(sem("hh_sb"), b + 1)
                moments(2, b, rope_a)

            def residual2_rest(b):
                dve.wait_ge(sem("norm_in"), 16)
                dve.wait_ge(sem("var"), norms(2, b))
                dve.wait_ge(sem("x1_beta"), b + 1)
                dve.scalar_tensor_tensor(out=rope_b[:, b, :], in0=rope_a[:, b, :], scalar=mv[:, 2, b, 0:1],
                                         in1=norm_s[:, 0, :], op0=ALU.subtract, op1=ALU.mult).then_inc(
                    sem("x2_step"), 1)
                dve.wait_ge(sem("x2_step"), 2 * b + 1)
                dve.wait_ge(sem("rstd"), norms(2, b))
                dve.scalar_tensor_tensor(out=acc[:, b, :], in0=rope_b[:, b, :], scalar=rstd[:, 2, b:b + 1],
                                         in1=x1[:, b, :], op0=ALU.mult, op1=ALU.add).then_inc(sem("x2_step"), 1)

            def route(b):
                dve.wait_ge(sem("logit_psum"), b + 1)
                pl = bank[4 * b][:, 0:E]
                dve.tensor_reduce(lmax[:, b:b + 1], pl, AX.X, ALU.max, negate=True).then_inc(sem("lmax"), 1)
                dve.wait_ge(sem("lmax"), b + 1)
                dve.tensor_scalar(lg[:, b, :], pl, lmax[:, b:b + 1], None, ALU.add).then_inc(sem("lshift"), 1)
                g, n = sem("gate_step"), 7 * b
                dve.wait_ge(sem("lexp"), b + 1)
                dve.tensor_reduce(lsum[:, b:b + 1], lge[:, b, :], AX.X, ALU.add).then_inc(g, 1)
                dve.wait_ge(g, n + 1)
                dve.reciprocal(lsum[:, b:b + 1], lsum[:, b:b + 1]).then_inc(g, 1)
                dve.wait_ge(g, n + 2)
                dve.tensor_scalar(lge[:, b, :], lge[:, b, :], lsum[:, b:b + 1], None, ALU.mult).then_inc(g, 1)
                dve.wait_ge(g, n + 3)
                dve.max(top8[:, b, :], lge[:, b, :]).then_inc(g, 1)
                dve.wait_ge(g, n + 4)
                dve.max_index(top_i[:, b, :], top8[:, b, :], lge[:, b, :]).then_inc(g, 1)
                dve.wait_ge(g, n + 5)
                dve.tensor_copy(top_f[:, b, :], top_i[:, b, :]).then_inc(g, 1)
                dve.wait_ge(g, n + 6)
                if b == 0:
                    dve.wait_ge(sem("iota_set"), 1)
                dve.tensor_scalar(pick[:, 1, b, :], iota8[:, :], top_f[:, b, 1:2], None, ALU.is_equal).then_inc(g, 1)
                dve.wait_ge(g, n + 7)
                dve.scalar_tensor_tensor(out=pick[:, 0, b, :], in0=iota8[:, :], scalar=top_f[:, b, 0:1],
                                         in1=pick[:, 1, b, :], op0=ALU.is_equal, op1=ALU.add).then_inc(
                    sem("pick"), 1)
                dve.wait_ge(sem("pick"), b + 1)
                dve.tensor_copy(picked[:, b, :], pick[:, 0, b, :]).then_inc(sem("picked"), 1)
                dve.tensor_tensor(gatep[:, b, :], lge[:, b, :], pick[:, 0, b, :], ALU.mult).then_inc(sem("gatep"), 1)

            dve.memset(band[:, :, :], 0.0).then_inc(sem("band_clear"), 1)
            bias_rest()
            dve.wait_ge(sem("x_in"), 16)
            moments(0, 0, x_s)
            moments(0, 1, x_s)
            normalise(0, 0, x_s, xn)
            normalise(0, 1, x_s, xn)
            dve.wait_ge(sem("rope_in"), 16)
            rotate("k", 0, 0, 2, kr)
            rotate("k", 1, 0, 2, kr)
            rotate("q", 0, 2, 0, qr, before="k")
            rotate("q", 1, 2, 0, qr, before="k")
            row_maxima(0, range(G))
            divide(0, (0, 1))
            probs_transposed(0, 0)
            divide(0, (2,))
            probs_transposed(0, 1)
            divide(0, (3,))
            row_maxima(1, (0,))
            probs_transposed(0, 2)
            row_maxima(1, (1,))
            probs_transposed(0, 3)
            row_maxima(1, (2, 3))
            mixed1(0)
            divide(1, range(G))
            residual1(0)
            normalise(1, 0, x1, xn)
            mixed1(1)
            beta_logit(0)
            beta(0)
            residual1(1)
            normalise(1, 1, x1, xn)
            rotate("q2", 0, 1, 2, qr, before="q")
            beta_logit(1)
            scans(0, (0, 1))
            beta(1)
            scans(0, (2, 3))
            rotate("k2", 0, 2, 2, kr, before="q2")
            scans(0, (4, 5, 6, 7))
            rotate("q2", 1, 1, 2, qr, before="q")
            linear("q2T", 0, 0, qT)
            linear("k2T", 0, 1, kT)
            scans(1, (0, 1, 2, 3))
            rotate("k2", 1, 2, 2, kr, before="q2")
            scans(1, (4, 5))
            gate_scores(0)
            scans(1, (6, 7))
            divide2(0)
            linear("q2T", 1, 0, qT)
            linear("k2T", 1, 1, kT)
            residual2(0)
            gate_scores(1)
            residual2_rest(0)
            divide2(1)
            moments(3, 0, acc)
            normalise(3, 0, acc, xn)
            residual2(1)
            residual2_rest(1)
            moments(3, 1, acc)
            normalise(3, 1, acc, xn)
            route(0)
            route(1)

            dve.wait_ge(sem("rank_psum"), 1)
            dve.scalar_tensor_tensor(out=place[:, 0].rearrange("p b e -> p (b e)"), in0=bank[7][:, 0:NB * E],
                                     scalar=float(FIRST_SLOT), in1=pick[:, 0, :, :].rearrange("p b e -> p (b e)"),
                                     op0=ALU.add, op1=ALU.mult).then_inc(sem("place_step"), 1)
            dve.tensor_reduce(most[:, 0:1], bank[7][:, NB * E:(NB + 1) * E], AX.X, ALU.max).then_inc(
                sem("place_step"), 1)
            dve.wait_ge(sem("place_step"), 1)
            dve.wait_ge(sem("iota_set"), 2)

            def one_hot(n):
                if n >= 2:
                    dve.wait_ge(sem("back_psum"), n - 1)
                turn, e = divmod(n, E)
                for b in range(NB):
                    ins = dve.tensor_scalar(onehot[:, n % 2, b, :], slot_no[:, :], place[:, turn, b, e:e + 1], None,
                                            ALU.is_equal)
                ins.then_inc(sem("onehot"), 1)

            def one_hot_pair(p):
                if p >= 2:
                    dve.wait_ge(sem("gather_psum"), 2 * (p - 1))
                for i in range(2):
                    turn, e = divmod(2 * p + i, E)
                    for b in range(NB):
                        ins = dve.tensor_scalar(onehot_pair[:, p % 2, b, i * SLOTS:(i + 1) * SLOTS], slot_no[:, :],
                                                place[:, turn, b, e:e + 1], None, ALU.is_equal)
                ins.then_inc(sem("onehot_pair"), 1)

            def experts(turn):
                for e in range(E):
                    n = turn * E + e
                    s = n % RING
                    for half in range(2):
                        dve.wait_ge(sem("w2_hi"), 2 * n + half + 1)
                        rows = slice(4 * half, 4 * half + 4)
                        dve.tensor_tensor(w2_lo[:, rows, :], w2_s[s][:, rows, :], w2_hi[:, rows, :].bitcast(F32),
                                          ALU.subtract).then_inc(sem("w2_split"), 1)
                    for half in range(2):
                        dve.wait_ge(sem("hid_hi"), 2 * n + half + 1)
                        rows = slice(4 * half, 4 * half + 4)
                        dve.tensor_tensor(hid_lo[:, rows, :], hid[:, rows, :], hid_hi[:, rows, :].bitcast(F32),
                                          ALU.subtract).then_inc(sem("hid_lo"), 1)
                    if e < E - 2:
                        one_hot(n + 2)
                        if e % 2 == 0:
                            one_hot_pair(n // 2 + 1)
                    dve.wait_ge(sem("y_hi"), n + 1)
                    dve.scalar_tensor_tensor(out=y_lo[:, :], in0=bank[6][:, :], scalar=slot_gate[:, n % 3:n % 3 + 1],
                                             in1=y_hi[:, :].bitcast(F32), op0=ALU.mult,
                                             op1=ALU.subtract).then_inc(sem("y_lo"), 1)

            one_hot_pair(0)
            one_hot(0)
            for k in range(3):
                src = gatep if k == 0 else g_rest
                dve.tensor_copy(gate_part[:, k], src[:, :, :]).then_inc(sem("gate_parts"), 1)
                dve.wait_ge(sem("gate_parts"), k + 1)
                if k < 2:
                    dve.tensor_tensor(g_rest[:, :, :], src[:, :, :], gate_part[:, k], ALU.subtract).then_inc(
                        sem("g_rest"), 1)
                    dve.wait_ge(sem("g_rest"), k + 1)
            one_hot(1)
            dve.tensor_scalar(place[:, 1], place[:, 0], -float(SLOTS), None, ALU.add).then_inc(sem("place_step"), 1)
            dve.wait_ge(sem("place_step"), 3)
            dve.tensor_scalar(most[:, 1:2], most[:, 0:1], float(SLOTS), None, ALU.is_gt).then_inc(sem("place_step"), 1)
            dve.wait_ge(sem("place_step"), 4)
            dve.tensor_copy(overflow[:, :], most[:, 1:2]).then_inc(sem("overflow_set"), 1)
            experts(0)
            dve.wait_ge(sem("overflow_set"), 1)
            with dve.If(dve.value_load(overflow[0:1, 0:1], min_val=0, max_val=1) > 0):
                one_hot_pair(E // 2)
                one_hot(E)
                one_hot(E + 1)
                experts(1)
            for b in range(NB):
                dve.wait_ge(sem("sum_psum"), b + 1)
                dve.tensor_tensor(acc[:, b, :], bank[4 + b][:, :], acc[:, b, :], ALU.add).then_inc(sem("result"), 1)


def kernel(**inputs):
    import numpy as np
    import concourse.bacc as bacc
    from concourse.bass_utils import run_bass_kernel_spmd

    i = {k: np.asarray(v) for k, v in inputs.items()}

    def rows(w):
        return np.ascontiguousarray(w.reshape(-1, P, w.shape[-1]).transpose(1, 0, 2))

    half = HD // 2
    freq = (1.0 / 10000.0 ** (np.arange(half, dtype=np.float32) / half)).astype(np.float32)
    ang = np.arange(P, dtype=np.float32)[:, None] * freq[None, :]
    cos = np.concatenate([np.cos(ang), np.cos(ang)], 1)
    sin = np.concatenate([-np.sin(ang), np.sin(ang)], 1)
    scale = HD ** -0.5
    rope = np.stack([cos * scale, sin * scale, cos, sin], 1).astype(np.float32)

    arrays = {
        "x": np.ascontiguousarray(i["x"].transpose(1, 0, 2)),
        "ctx_t": rows(i["ctx_1024"][:, :P].transpose(2, 0, 1).reshape(D, NB * P)),
        "rope": rope,
        "wk": rows(i["L0_xattn_k_w"].T), "wv": rows(i["L0_xattn_v_w"].T),
        "wq": rows(i["L0_xattn_q_w"].T), "wo": rows(i["L0_xattn_o_w"].T),
        "aq": rows(i["L0_attn_Wq"]), "ak": rows(i["L0_attn_Wk"]),
        "av": rows(i["L0_attn_Wv"]), "ao": rows(i["L0_attn_Wo"]),
        "wbeta": rows(i["L0_attn_Wbeta"]),
        "bbeta": np.ascontiguousarray(i["L0_attn_bbeta"].reshape(H * C, 1)),
        "biases": np.stack([i["L0_xattn_k_b"], i["L0_xattn_v_b"], i["L0_xattn_q_b"], i["L0_xattn_o_b"],
                            i["L0_attn_bo"]]),
        "norm_rows": np.stack([i["L0_attn_ln_gamma"], i["L0_attn_ln_beta"]]),
        "gate_w": rows(i["L0_ffn_gate_w"].T),
        "gate_b": np.ascontiguousarray(i["L0_ffn_gate_b"].reshape(1, E)),
        "w1": np.ascontiguousarray(i["L0_ffn_w1"].reshape(E, DC, P, FF).transpose(0, 2, 1, 3)),
        "b1": np.ascontiguousarray(i["L0_ffn_b1"].reshape(E, FC, P).transpose(2, 0, 1)),
        "w2": np.ascontiguousarray(i["L0_ffn_w2"].reshape(E, FC, P, D).transpose(0, 2, 1, 3)),
        "b2": np.ascontiguousarray(i["L0_ffn_b2"]),
    }
    nc = bacc.Bacc("TRN2", target_bir_lowering=False, num_devices=1)
    args = [nc.dram_tensor(n, a.shape, mybir.dt.from_np(a.dtype), kind="ExternalInput").ap()
            for n, a in arrays.items()]
    out = nc.dram_tensor("out", (P, NB, D), F32, kind="ExternalOutput").ap()
    build(nc, *args, out)
    r = run_bass_kernel_spmd(nc, [arrays], core_ids=[0])
    return np.ascontiguousarray(r.results[0]["out"].transpose(1, 0, 2))
```
